# Optimizing a Trainium2 kernel written in Bass

```python
import numpy as np
import jax
import jax.numpy as jnp

def _softmax(x, axis=-1):
    return jax.nn.softmax(x, axis=axis)

def _gelu(x):
    return jax.nn.gelu(x, approximate=True)

def _silu(x):
    return jax.nn.silu(x)

def _sigmoid(x):
    return jax.nn.sigmoid(x)

def _layernorm(x, axis=-1, eps=1e-05):
    m = jnp.mean(x, axis=axis, keepdims=True)
    v = jnp.var(x, axis=axis, keepdims=True)
    return (x - m) / jnp.sqrt(v + eps)

def _scatter_add(tgt, idx, src, axis=0):
    return tgt.at[idx].add(src)

def _segment_sum(src, seg, n):
    return jax.ops.segment_sum(src, seg, n)
kernel_name = 'mk_seq_postln_d1_jaxref_r8_15bff9'

def setup_inputs(seed: int=0):
    np.random.seed(seed)
    _w = jnp.asarray

    def _L0_attn_setup():
        import jax, jax.numpy as jnp
        import numpy as np
        B, S, E, H = (2, 256, 128, 16)
        D = E // H
        key = jax.random.key(seed)
        k1, k2, k3 = jax.random.split(key, 3)
        x = jax.random.normal(k1, (B, S, E), dtype=jnp.float32)
        lim_qkv = np.sqrt(6.0 / (E + 3 * E)).astype(np.float32)
        lim_out = np.sqrt(6.0 / (E + E)).astype(np.float32)
        w_qkv = jax.random.uniform(k2, (E, 3 * E), jnp.float32, -lim_qkv, lim_qkv)
        w_out = jax.random.uniform(k3, (E, E), jnp.float32, -lim_out, lim_out)
        return {'x': x, 'w_qkv': w_qkv, 'w_out': w_out}
    _L0_attn_in = _L0_attn_setup()

    def _L0_ffn_setup():
        import jax, jax.numpy as jnp
        import numpy as np
        B, S = (4, 256)
        D_MODEL, D_FF, N_EXPERTS, TOP_K = (128, 512, 8, 2)
        T = B * S
        CAPACITY_FACTOR, MIN_CAP = (1.25, 4)
        CAP = max(int(CAPACITY_FACTOR * (T * TOP_K / N_EXPERTS)), MIN_CAP)
        key = jax.random.key(seed)
        ks = jax.random.split(key, 6)

        def w(k, shape, fan):
            return jax.random.normal(k, shape, jnp.float32) * fan ** (-0.5)
        return {'x': jax.random.normal(ks[0], (B, S, D_MODEL), jnp.float32), 'Wr': w(ks[1], (D_MODEL, N_EXPERTS), D_MODEL), 'W1': w(ks[2], (N_EXPERTS, D_MODEL, D_FF), D_MODEL), 'b1': jnp.zeros((N_EXPERTS, D_FF), jnp.float32), 'W2': w(ks[3], (N_EXPERTS, D_FF, D_MODEL), D_FF), 'b2': jnp.zeros((N_EXPERTS, D_MODEL), jnp.float32), 'fw1': w(ks[4], (D_MODEL, D_FF), D_MODEL), 'fb1': jnp.zeros((D_FF,), jnp.float32), 'fw2': w(ks[5], (D_FF, D_MODEL), D_FF), 'fb2': jnp.zeros((D_MODEL,), jnp.float32)}
    _L0_ffn_in = _L0_ffn_setup()
    _d = {'L0_attn_x': _L0_attn_in['x'], 'L0_attn_w_qkv': _L0_attn_in['w_qkv'], 'L0_attn_w_out': _L0_attn_in['w_out'], 'L0_ffn_Wr': _L0_ffn_in['Wr'], 'L0_ffn_W1': _L0_ffn_in['W1'], 'L0_ffn_b1': _L0_ffn_in['b1'], 'L0_ffn_W2': _L0_ffn_in['W2'], 'L0_ffn_b2': _L0_ffn_in['b2'], 'L0_ffn_fw1': _L0_ffn_in['fw1'], 'L0_ffn_fb1': _L0_ffn_in['fb1'], 'L0_ffn_fw2': _L0_ffn_in['fw2'], 'L0_ffn_fb2': _L0_ffn_in['fb2']}
    _x0 = _d['L0_attn_x']
    _d['L0_attn_x'] = jax.random.normal(jax.random.fold_in(jax.random.key(seed), 1), (16, 512, 128), dtype=_x0.dtype)
    del _x0
    return _d

def reference(L0_attn_x, L0_attn_w_qkv, L0_attn_w_out, L0_ffn_Wr, L0_ffn_W1, L0_ffn_b1, L0_ffn_W2, L0_ffn_b2, L0_ffn_fw1, L0_ffn_fb1, L0_ffn_fw2, L0_ffn_fb2):

    def _L0_attn_ref(x, w_qkv, w_out):
        import jax, jax.numpy as jnp
        import numpy as np
        B, S, E, H = (2, 256, 128, 16)
        D = E // H
        b, s, e = x.shape
        qkv = jnp.einsum('bse,ef->bsf', x, w_qkv)
        qkv = qkv.reshape(b, s, 3, H, D).transpose(2, 0, 3, 1, 4)
        q, k, v = (qkv[0], qkv[1], qkv[2])
        scale = 1.0 / np.sqrt(D).astype(np.float32)
        scores = jnp.einsum('bhsd,bhtd->bhst', q, k) * scale
        attn = jax.nn.softmax(scores, axis=-1)
        out = jnp.einsum('bhst,bhtd->bhsd', attn, v)
        out = out.transpose(0, 2, 1, 3).reshape(b, s, e)
        return jnp.einsum('bse,ef->bsf', out, w_out)

    def _L0_ffn_ref(x, Wr, W1, b1, W2, b2, fw1, fb1, fw2, fb2):
        import jax, jax.numpy as jnp
        import numpy as np
        B, S = (4, 256)
        D_MODEL, D_FF, N_EXPERTS, TOP_K = (128, 512, 8, 2)
        T = B * S
        CAPACITY_FACTOR, MIN_CAP = (1.25, 4)
        CAP = max(int(CAPACITY_FACTOR * (T * TOP_K / N_EXPERTS)), MIN_CAP)
        Bx, Sx, D = x.shape
        Tn = Bx * Sx
        xf = x.reshape(Tn, D)
        logits = xf @ Wr
        probs = jax.nn.softmax(logits, axis=-1)
        scores, experts = jax.lax.top_k(probs, TOP_K)
        scores = scores / jnp.maximum(scores.sum(-1, keepdims=True), 1e-09)
        y_fb = jax.nn.gelu(xf @ fw1 + fb1, approximate=False) @ fw2 + fb2
        y = jnp.zeros_like(xf)
        fb_mask = jnp.zeros((Tn,), bool)
        for e in range(N_EXPERTS):
            assign = experts == e
            w_e = jnp.where(assign, scores, 0.0).sum(-1)
            eligible = assign.any(-1) & ~fb_mask
            rank = jnp.cumsum(eligible.astype(jnp.int32)) - 1
            keep = eligible & (rank < CAP)
            overflow = eligible & ~keep
            fb_mask = fb_mask | overflow
            y = jnp.where(overflow[:, None], y_fb, y)
            idx = jnp.nonzero(keep, size=CAP, fill_value=0)[0]
            valid = jnp.arange(CAP) < keep.sum()
            h = jax.nn.gelu(xf[idx] @ W1[e] + b1[e], approximate=False)
            y_e = h @ W2[e] + b2[e]
            y = y.at[idx].add(y_e * (w_e[idx] * valid)[:, None])
        return y.reshape(Bx, Sx, D)
    x = L0_attn_x
    x = _layernorm(x + _L0_attn_ref(x, L0_attn_w_qkv, L0_attn_w_out), axis=-1)
    x = _layernorm(x + _L0_ffn_ref(x, L0_ffn_Wr, L0_ffn_W1, L0_ffn_b1, L0_ffn_W2, L0_ffn_b2, L0_ffn_fw1, L0_ffn_fb1, L0_ffn_fw2, L0_ffn_fb2), axis=-1)
    return x

_drawn_inputs = setup_inputs


def setup_inputs(seed=0):
    import zlib

    import numpy as np

    out = dict(_drawn_inputs(seed))
    spreads = {'L0_ffn_b1': (0.0, 0.46),
     'L0_ffn_b2': (0.0, 0.316),
     'L0_ffn_fb1': (0.0, 0.1),
     'L0_ffn_fb2': (0.0, 0.1)}
    factors = {}
    for name, (base, spread) in spreads.items():
        noise = np.random.default_rng([zlib.crc32(name.encode()), seed]).standard_normal(out[name].shape)
        drawn = base * np.exp(spread * noise) if base else spread * noise
        out[name] = jnp.asarray(drawn.astype(out[name].dtype))
    for name, factor in factors.items():
        out[name] = (out[name] * factor).astype(out[name].dtype)
    return out
```

```python
from contextlib import ExitStack

import concourse.bass as bass
from concourse import mybir

F32 = mybir.dt.float32
BF16 = mybir.dt.bfloat16
U32 = mybir.dt.uint32
ALU = mybir.AluOpType
ACT = mybir.ActivationFunctionType
AX = mybir.AxisListType

P = 128
BATCH, S, E = 16, 512, 128
H = 16
D = E // H
ST = S // P
SCALE = 1.0 / float(D) ** 0.5
PARTS = 3
QK_ROWS = PARTS * PARTS * D
ROWS = QK_ROWS + PARTS
HALF = H // 2
GROUP = 4
NG = H // GROUP
VW = 32
ZERO_ROWS = 8
BANKS = 3
TILES_B = H * ST
ORDER = (((0,), (0,)), ((1,), (1, 2)), ((2, 3), (3,)))
UNITS = NG * ST
EPS = 1e-5


def attention(nc, ctx, block, x_dram, wqkv_dram, wout_dram, ident_dram, z, moments, y_rows):

    def sb(name, shape, dt):
        return ctx.enter_context(nc.sbuf_tensor(name, shape, dt))

    def ps(name, shape):
        return ctx.enter_context(nc.psum_tensor(name, shape, F32))

    def sem(name):
        return ctx.enter_context(nc.semaphore(name))

    parts_dram = nc.dram_tensor("qk_parts", [2, 2, PARTS, D, H, S], BF16, kind="Internal").ap()

    w_qkv = sb("w_qkv", [P, 3 * E], F32)
    w_out = sb("w_out", [P, E], F32)
    ident = sb("ident", [P, P], F32)
    x_stage = [sb(f"x_stage{i}", [P, ST, E], F32) for i in range(2)]
    xT = [sb(f"xT{i}", [P, S], F32) for i in range(2)]
    part = [sb(f"part{i}", [P, PARTS, S], BF16) for i in range(2)]
    rest = [sb(f"rest{i}", [P, S], F32) for i in range(2)]
    q_stack = [sb(f"q_stack{i}", [P, H, S], BF16) for i in range(2)]
    k_stack = [sb(f"k_stack{i}", [P, H, S], BF16) for i in range(2)]
    v_ones = [sb(f"v_ones{i}", [P, ST, H, VW], F32) for i in range(2)]
    neg_max = [sb(f"neg_max{i}", [P, HALF, ST], F32) for i in range(2)]
    max_part = [sb(f"max_part{i}", [HALF * ST, PARTS, P], BF16) for i in range(2)]
    max_rest = [sb(f"max_rest{i}", [HALF * ST, 2, P], F32) for i in range(2)]
    probs = [sb(f"probs{i}", [P, GROUP, S], F32) for i in range(2)]
    out_raw = [sb(f"out_raw{i}", [P, S], F32) for i in range(2)]
    inv_den = sb("inv_den", [P, ST, GROUP], F32)
    out_tok = [sb(f"out_tok{i}", [P, ST, H, D], F32) for i in range(2)]
    tile_stats = sb("tile_stats", [P, ST, 6], F32)
    tile_moments = sb("tile_moments", [P, ST, 2], F32)
    eps_col = sb("eps_col", [P, ST, 2], F32)
    z_stage = sb("z_stage", [P, ST, E], F32)
    outT = sb("outT", [P, S], F32)

    zero = sb("zero", [P, ZERO_ROWS * E], F32)

    max_ps = ps("max_ps", [P, 3, S])
    exp_ps = ps("exp_ps", [P, 3, S])
    pv_ps = ps("pv_ps", [P, S])
    misc_ps = ps("misc_ps", [P, S])

    load_w = sem("load_w")
    load_x = [sem("load_x0"), sem("load_x1")]
    load_z = sem("load_z")
    ones_set = sem("ones_set")
    zeros_out = sem("zeros_out")
    scores_a = sem("scores_a")
    max_done = sem("max_done")
    scores_b = sem("scores_b")
    exp_done = sem("exp_done")
    pv_done = sem("pv_done")
    raw_done = sem("raw_done")
    misc_wr = sem("misc_wr")
    misc_rd = sem("misc_rd")
    part1_done = sem("part1_done")
    parts_done = sem("parts_done")
    part2_done = sem("part2_done")
    parts_out = sem("parts_out")
    stack_in = [[sem(f"stack_in{c}{h}") for h in range(2)] for c in range(2)]
    mpart1 = sem("mpart1")
    mpart2 = sem("mpart2")
    mpart3 = sem("mpart3")
    mrow_in = [sem("mrow_in0"), sem("mrow_in1")]
    stats_done = sem("stats_done")
    aggr_done = sem("aggr_done")
    moments_kept = sem("moments_kept")
    z_kept = sem("z_kept")
    inv_done = sem("inv_done")

    x_tok = x_dram.rearrange("b (t p) e -> b p t e", p=P)

    TASK = {0: "max1", 1: "norm3", 2: "xT", 3: "outT", 4: "proj", 5: "norm0", 6: "q", 7: "k", 8: "v",
            9: "norm1", 10: "max0", 13: "norm2"}
    PRO = 8

    def before_bank(n):
        return n - BANKS + 1 if n >= BANKS else n - (TILES_B - 1) % BANKS if n == 0 else n - BANKS

    def has(task, b):
        if b is None:
            return True
        if task in ("norm3", "outT", "proj"):
            return b > 0
        if task in ("xT", "q", "k"):
            return b < BATCH - 2
        if task in ("max0", "v"):
            return b < BATCH - 1
        return True

    def tasks_before(b, known, u):
        n = sum(1 for v in TASK if v < u and has(TASK[v], known))
        if known is None or known >= 1:
            late = 0
            if known is not None and known == BATCH - 1:
                late = 3
            return 12 * b + 5 - late + n
        return PRO + n

    def batches(engine, body):
        for b in (0, 1):
            body(b, b % 2, b)
        with engine.Fori(1, BATCH // 2 - 1) as i:
            for c in (0, 1):
                body(2 * i + c, c, None)
        for b in (BATCH - 2, BATCH - 1):
            body(b, b % 2, b)

    @block.sync
    def _(sp):
        sp.dma_start(w_qkv[:, :], wqkv_dram).then_inc(load_w, 16)
        sp.dma_start(w_out[:, :], wout_dram).then_inc(load_w, 16)
        sp.dma_start(ident[:, :], ident_dram).then_inc(load_w, 16)
        for b in (0, 1):
            sp.dma_start(x_stage[b][:, :, :], x_tok[b]).then_inc(load_x[b], 16)
        for b in range(BATCH):
            sp.dma_start(z[:, ST * b:ST * (b + 1), :], x_tok[b]).then_inc(load_z, 16)

        def parts_to_dram(b, c):
            sp.wait_ge(parts_done, 2 * b + 2)
            for qk in range(2):
                for n in range(PARTS):
                    sp.dma_start(parts_dram[c, qk, n].rearrange("d h s -> h d s"),
                                 part[qk][:, n, :]).then_inc(parts_out, 16)

        def stack_load(b, c, half):
            sp.wait_ge(parts_out, 96 * b + 96)
            hs = slice(half * HALF, (half + 1) * HALF)
            for n in range(PARTS):
                rows = slice(n * PARTS * D, (n + 1) * PARTS * D)
                for r in range(PARTS):
                    sub = slice((n * PARTS + r) * D, (n * PARTS + r + 1) * D)
                    sp.dma_start(q_stack[c][sub, hs, :], parts_dram[c, 0, n, :, hs, :]).then_inc(stack_in[c][half], 16)
                sp.dma_start(k_stack[c][rows, hs, :],
                             parts_dram[c, 1].rearrange("n d h s -> (n d) h s")[:, hs, :]).then_inc(stack_in[c][half], 16)

        def rows(b, c, half):
            sp.wait_ge(mpart3, 2 * b + half + 1)
            for n in range(PARTS):
                sp.dma_start(q_stack[c][QK_ROWS + n:QK_ROWS + n + 1, half * HALF:(half + 1) * HALF, :],
                               max_part[half][:, n, :]).then_inc(mrow_in[half], 16)

        sp.wait_ge(ones_set, 2)
        for b in (0, 1):
            parts_to_dram(b, b)
            stack_load(b, b, 0)
            stack_load(b, b, 1)
        rows(0, 0, 0)

        def body(b, c, known):
            rows(b, c, 1)
            if known is None or known < BATCH - 2:
                sp.dma_start(x_stage[c][:, :, :], x_tok[b + 2]).then_inc(load_x[c], 16)
                parts_to_dram(b + 2, c)
                sp.wait_ge(scores_b, TILES_B * b + TILES_B // 2)
                stack_load(b + 2, c, 0)
            if known is None or known < BATCH - 1:
                rows(b + 1, 1 - c, 0)
            if known is None or known < BATCH - 2:
                sp.wait_ge(scores_b, TILES_B * b + TILES_B)
                stack_load(b + 2, c, 1)

        batches(sp, body)

    @block.gpsimd
    def _(pool):
        for n, tile in enumerate([k_stack[0][64:P, :, :], k_stack[1][64:P, :, :],
                                  v_ones[0][:, :, :, :], v_ones[1][:, :, :, :]]):
            nc.gpsimd.memset(tile, 1.0).then_inc(ones_set, 1)
            pool.wait_ge(ones_set, n + 1)

        def split(b, qk):
            n = 2 * b + qk
            pool.wait_ge(part2_done, n + 1)
            nc.gpsimd.tensor_tensor(part[qk][:, 2, :], rest[qk][:, :], part[qk][:, 1, :],
                                    ALU.subtract).then_inc(parts_done, 1)

        for b in (0, 1):
            for qk in (0, 1):
                split(b, qk)
        nc.gpsimd.memset(zero[:, :], 0.0).then_inc(ones_set, 1)
        pool.wait_ge(ones_set, 5)
        zero_view = y_rows.rearrange("(n p r) e -> n p (r e)", p=P, r=ZERO_ROWS)
        with pool.Fori(0, 2 * BATCH * S // (P * ZERO_ROWS)) as i:
            pool.dma_start(zero_view[i], zero[:, :]).then_inc(zeros_out, 16)

        def body(b, c, known):
            if known is None or known < BATCH - 2:
                for qk in (0, 1):
                    split(b + 2, qk)

        batches(pool, body)
        pool.wait_ge(zeros_out, 16 * 2 * BATCH * S // (P * ZERO_ROWS))

    @block.tensor
    def _(pe):
        def misc_turn(count):
            pe.wait_ge(misc_rd, count)

        def t_xT(b, c, count):
            if isinstance(b, int):
                pe.wait_ge(load_x[c], 16 * (b // 2) + 16)
            else:
                pe.wait_ge(load_x[c], 8 * (b - c) + 16)
            misc_turn(count)
            for t in range(ST):
                last = nc.tensor.transpose(misc_ps[:, t * P:(t + 1) * P], x_stage[c][:, t, :], ident[:, :])
            last.then_inc(misc_wr, 1)

        def t_qk(b, c, count, qk):
            misc_turn(count)
            nc.tensor.matmul(misc_ps[:, :], w_qkv[:, qk * E:(qk + 1) * E], xT[c][:, :],
                             start=True, stop=True).then_inc(misc_wr, 1)

        def t_v(b, c, count):
            misc_turn(count)
            for t in range(ST):
                last = nc.tensor.matmul(misc_ps[:, t * P:(t + 1) * P], xT[c][:, t * P:(t + 1) * P],
                                        w_qkv[:, 2 * E:3 * E], start=True, stop=True)
            last.then_inc(misc_wr, 1)

        def t_max(b, half, count):
            pe.wait_ge(max_done, 64 * b + 32 * half + 32)
            misc_turn(count)
            nc.tensor.transpose(misc_ps[0:HALF * ST, 0:P], neg_max[half][:, :, :].rearrange("p h t -> p (h t)"),
                                ident[:, :]).then_inc(misc_wr, 1)

        def t_norm(b, g, count):
            pe.wait_ge(raw_done, NG * b + g + 1)
            misc_turn(count)
            for t in range(ST):
                last = nc.tensor.transpose(misc_ps[:, t * P:(t + 1) * P], out_raw[g % 2][:, t * P:(t + 1) * P],
                                           ident[:, :])
            last.then_inc(misc_wr, 1)

        def t_outT(b, c, count):
            misc_turn(count)
            for t in range(ST):
                last = nc.tensor.transpose(misc_ps[:, t * P:(t + 1) * P],
                                           out_tok[c][:, t, :, :].rearrange("p h d -> p (h d)"), ident[:, :])
            last.then_inc(misc_wr, 1)

        def t_proj(b, count):
            misc_turn(count)
            for t in range(ST):
                last = nc.tensor.matmul(misc_ps[:, t * P:(t + 1) * P], outT[:, t * P:(t + 1) * P], w_out[:, :],
                                        start=True, stop=True)
            last.then_inc(misc_wr, 1)

        def score_max(b, c, h, tiles=range(ST)):
            if h % HALF == 0 and 0 in tiles:
                pe.wait_ge(stack_in[c][h // HALF], 96 * (b - c) + 192)
            for t in tiles:
                n = ST * h + t
                if not isinstance(b, int) or b > 0 or n >= BANKS:
                    pe.wait_ge(max_done, TILES_B * b + before_bank(n))
                nc.tensor.matmul(max_ps[:, n % BANKS, :], q_stack[c][0:QK_ROWS, h, t * P:(t + 1) * P],
                                 k_stack[c][0:QK_ROWS, h, :], start=True, stop=True).then_inc(scores_a, 1)

        def score_exp(b, c, u, heads):
            g, t = u // ST, u % ST
            if u % (UNITS // 2) == 0 and 0 in heads:
                pe.wait_ge(mrow_in[u // (UNITS // 2)], 48 * b + 48)
            for j in heads:
                h = g * GROUP + j
                n = GROUP * u + j
                if not isinstance(b, int) or b > 0 or n >= BANKS:
                    pe.wait_ge(exp_done, TILES_B * b + before_bank(n))
                nc.tensor.matmul(exp_ps[:, n % BANKS, :], k_stack[c][0:ROWS, h, t * P:(t + 1) * P],
                                 q_stack[c][0:ROWS, h, :], start=True, stop=True).then_inc(scores_b, 1)

        def pv(b, v_slot, u):
            g, t = u // ST, u % ST
            pe.wait_ge(exp_done, TILES_B * b + GROUP * u + GROUP)
            if t == 0 and (not isinstance(b, int) or (b, g) != (0, 0)):
                pe.wait_ge(raw_done, NG * b + g)
            for j in range(GROUP):
                mm = nc.tensor.matmul(pv_ps[VW * j:VW * (j + 1), :], v_ones[v_slot][:, t, g * GROUP + j, :],
                                      probs[u % 2][:, j, :], start=(t == 0), stop=(t == ST - 1))
            mm.then_inc(pv_done, 1)

        pe.wait_ge(load_w, 48)
        for b in (0, 1):
            n = 4 * b
            t_xT(b, b, n)
            t_qk(b, b, n + 1, 0)
            t_qk(b, b, n + 2, 1)
            if b == 0:
                t_v(b, b, n + 3)
        for h in range(H):
            score_max(0, 0, h)
            if h == 10:
                t_max(0, 0, PRO - 1)

        def body(b, c, known):
            for u in range(UNITS):
                ahead = known is None or known < BATCH - 1
                for tiles, heads in ORDER:
                    score_exp(b, c, u, heads)
                    if ahead:
                        score_max(b + 1, 1 - c, u, tiles)
                count = tasks_before(b, known, u)
                task = TASK.get(u)
                if task is not None and has(task, known):
                    if task == "xT":
                        t_xT(b + 2, c, count)
                    elif task == "q":
                        t_qk(b + 2, c, count, 0)
                    elif task == "k":
                        t_qk(b + 2, c, count, 1)
                    elif task == "v":
                        t_v(b + 1, 1 - c, count)
                    elif task == "max0":
                        t_max(b + 1, 0, count)
                    elif task == "max1":
                        t_max(b, 1, count)
                    elif task == "norm3":
                        t_norm(b - 1, 3, count)
                    elif task == "outT":
                        t_outT(b - 1, 1 - c, count)
                    elif task == "proj":
                        t_proj(b - 1, count)
                    else:
                        t_norm(b, int(task[-1]), count)
                if u > 0:
                    pv(b, c, u - 1)
                elif known is None or known > 0:
                    pv(b - 1, 1 - c, UNITS - 1)

        batches(pe, body)
        end = tasks_before(BATCH - 1, BATCH - 1, UNITS)
        pv(BATCH - 1, 1, UNITS - 1)
        t_norm(BATCH - 1, 3, end)
        t_outT(BATCH - 1, 1, end + 1)
        t_proj(BATCH - 1, end + 2)

    @block.scalar
    def _(act):
        def exps(b, u):
            if not isinstance(b, int) or 16 * b + u >= 2:
                act.wait_ge(pv_done, 16 * b + u - 1)
            for j in range(GROUP):
                n = GROUP * u + j
                act.wait_ge(scores_b, TILES_B * b + n + 1)
                nc.scalar.activation(probs[u % 2][:, j, :], exp_ps[:, n % BANKS, :], ACT.Exp,
                                     scale=SCALE).then_inc(exp_done, 1)

        def e_xT(b, c, count):
            act.wait_ge(misc_wr, count + 1)
            nc.scalar.copy(xT[c][:, :], misc_ps[:, :]).then_inc(misc_rd, 1)

        def e_part1(b, count, qk):
            act.wait_ge(misc_wr, count + 1)
            if not isinstance(b, int) or b >= 1:
                act.wait_ge(parts_out, 96 * b)
            nc.scalar.copy(part[qk][:, 0, :], misc_ps[:, :]).then_inc(part1_done, 1)

        def e_part2(b, count, qk):
            act.wait_ge(misc_rd, count + 1)
            nc.scalar.copy(part[qk][:, 1, :], rest[qk][:, :]).then_inc(part2_done, 1)

        def e_v(b, c, count):
            act.wait_ge(misc_wr, count + 1)
            nc.scalar.copy(v_ones[c][:, :, :, 0:D], misc_ps[:, :].rearrange("p (t h d) -> p t h d", t=ST, h=H)
                           ).then_inc(misc_rd, 1)

        def e_max(b, half, count):
            act.wait_ge(misc_wr, count + 1)
            if not isinstance(b, int) or b >= 1:
                act.wait_ge(mrow_in[half], 48 * b)
            nc.scalar.copy(max_part[half][:, 0, :], misc_ps[0:HALF * ST, 0:P]).then_inc(mpart1, 1)

        def e_outT(b, count):
            act.wait_ge(misc_wr, count + 1)
            nc.scalar.copy(outT[:, :], misc_ps[:, :]).then_inc(misc_rd, 1)

        def e_raw(b, g, count):
            act.wait_ge(pv_done, 16 * b + 4 * g + 4)
            act.wait_ge(misc_wr, count)
            nc.scalar.copy(out_raw[g % 2][:, :], pv_ps[:, :]).then_inc(raw_done, 1)

        act.wait_ge(ones_set, 4)
        for b in (0, 1):
            n = 4 * b
            e_xT(b, b, n)
            e_part1(b, n + 1, 0)
            e_part1(b, n + 2, 1)
            e_part2(b, n + 1, 0)
            e_part2(b, n + 2, 1)
            if b == 0:
                e_v(b, b, n + 3)
        e_max(0, 0, PRO - 1)

        def body(b, c, known):
            for u in range(UNITS):
                exps(b, u)
                count = tasks_before(b, known, u)
                task = TASK.get(u)
                if task is not None and has(task, known):
                    if task == "xT":
                        e_xT(b + 2, c, count)
                    elif task == "q":
                        e_part1(b + 2, count, 0)
                    elif task == "k":
                        e_part1(b + 2, count, 1)
                    elif task == "v":
                        e_v(b + 1, 1 - c, count)
                    elif task == "max0":
                        e_max(b + 1, 0, count)
                    elif task == "max1":
                        e_max(b, 1, count)
                    elif task == "outT":
                        e_outT(b - 1, count)
                if u in (7, 8) and has("q", known):
                    e_part2(b + 2, tasks_before(b, known, u - 1), u - 7)
                if u % ST == 0 and u > 0:
                    e_raw(b, u // ST - 1, tasks_before(b, known, {4: 0, 8: 2, 12: 6}[u]))
                elif u == 0 and (known is None or known > 0):
                    e_raw(b - 1, NG - 1, tasks_before(b, known, 0))

        batches(act, body)
        end = tasks_before(BATCH - 1, BATCH - 1, UNITS)
        e_raw(BATCH - 1, NG - 1, end)
        e_outT(BATCH - 1, end + 1)

    @block.vector
    def _(dve):
        def maxima(b, h):
            for t in range(ST):
                dve.wait_ge(scores_a, 64 * b + 4 * h + t + 1)
                if h % HALF == 0 and t == 0 and (not isinstance(b, int) or b >= 1):
                    dve.wait_ge(mpart1, 2 * b - 1 + h // HALF)
                nc.vector.tensor_reduce(neg_max[h // HALF][:, h % HALF, t:t + 1], max_ps[:, (ST * h + t) % BANKS, :], AX.X, ALU.max,
                                        negate=True).then_inc(max_done, 1)

        def d_rest1(b, qk):
            n = 2 * b + qk
            dve.wait_ge(part1_done, n + 1)
            if not isinstance(b, int) or b >= 1:
                dve.wait_ge(parts_done, n - 1)
            nc.vector.tensor_tensor(rest[qk][:, :], misc_ps[:, :], part[qk][:, 0, :], ALU.subtract
                                    ).then_inc(misc_rd, 1)

        def d_max(b, half, count):
            n = 2 * b + half
            dve.wait_ge(mpart1, n + 1)
            mp, mr = max_part[half], max_rest[half]
            nc.vector.tensor_tensor(mr[:, 0, :], misc_ps[0:HALF * ST, 0:P], mp[:, 0, :], ALU.subtract).then_inc(misc_rd, 1)
            dve.wait_ge(misc_rd, count + 1)
            nc.vector.tensor_copy(mp[:, 1, :], mr[:, 0, :]).then_inc(mpart2, 1)
            dve.wait_ge(mpart2, n + 1)
            nc.vector.tensor_tensor(mp[:, 2, :], mr[:, 0, :], mp[:, 1, :], ALU.subtract).then_inc(mpart3, 1)

        def d_norm(b, c, g, count):
            n = NG * b + g
            dve.wait_ge(misc_wr, count + 1)
            view = misc_ps[:, :].rearrange("p (t j w) -> p t j w", t=ST, w=VW)
            nc.vector.reciprocal(inv_den[:, :, :], view[:, :, :, D]).then_inc(inv_done, 1)
            dve.wait_ge(inv_done, n + 1)
            nc.vector.tensor_tensor(out_tok[c][:, :, g * GROUP:(g + 1) * GROUP, :], view[:, :, :, 0:D],
                                    inv_den[:, :, :].unsqueeze(3).to_broadcast([P, ST, GROUP, D]), ALU.mult
                                    ).then_inc(misc_rd, 1)

        def d_z(b, count):
            dve.wait_ge(misc_wr, count + 1)
            zb = z[:, bass.ds(b * ST, ST), :]
            nc.vector.tensor_tensor(z_stage[:, :, :], zb, misc_ps[:, :].rearrange("p (t e) -> p t e", t=ST), ALU.add
                                    ).then_inc(misc_rd, 1)
            dve.wait_ge(misc_rd, count + 1)
            for t in range(ST):
                last = nc.vector.bn_stats(tile_stats[:, t, :], z_stage[:, t, :])
            last.then_inc(stats_done, 1)
            dve.wait_ge(stats_done, b + 1)
            nc.vector.tensor_scalar(zb, z_stage[:, :, :], 1.0, None, ALU.mult).then_inc(z_kept, 1)
            for t in range(ST):
                last = nc.vector.bn_aggr(tile_moments[:, t, :], tile_stats[:, t, :])
            last.then_inc(aggr_done, 1)
            dve.wait_ge(aggr_done, b + 1)
            nc.vector.tensor_tensor(moments[:, bass.ds(b * ST, ST), :], tile_moments[:, :, :], eps_col[:, :, :],
                                    ALU.add).then_inc(moments_kept, 1)

        nc.vector.memset(eps_col[:, :, 0:1], 0.0)
        nc.vector.memset(eps_col[:, :, 1:2], EPS)
        for b in (0, 1):
            for qk in (0, 1):
                d_rest1(b, qk)
        for h in range(H):
            maxima(0, h)
            if h == 10:
                d_max(0, 0, PRO - 1)
        dve.wait_ge(load_z, 16 * BATCH)

        def body(b, c, known):
            for u in range(UNITS):
                if known is None or known < BATCH - 1:
                    maxima(b + 1, u)
                count = tasks_before(b, known, u)
                task = TASK.get(u)
                if task is not None and has(task, known):
                    if task == "q":
                        d_rest1(b + 2, 0)
                    elif task == "k":
                        d_rest1(b + 2, 1)
                    elif task == "max0":
                        d_max(b + 1, 0, count)
                    elif task == "max1":
                        d_max(b, 1, count)
                    elif task == "norm3":
                        d_norm(b - 1, 1 - c, 3, count)
                    elif task == "proj":
                        d_z(b - 1, count)
                    elif task.startswith("norm"):
                        d_norm(b, c, int(task[-1]), count)

        batches(dve, body)
        end = tasks_before(BATCH - 1, BATCH - 1, UNITS)
        d_norm(BATCH - 1, 1, 3, end)
        d_z(BATCH - 1, end + 2)


TILES = BATCH * S // P
CHUNKS = BATCH
TOK = BATCH * S
FF, EXP, CAP = 512, 8, 320
FC = FF // P
SLOTS = EXP * CAP
SLOT_TILES = SLOTS // P
NOWHERE = 4096.0
BACK_AFTER = [e * CAP // (ST * P) if e < EXP else SLOT_TILES // ST for e in range(EXP + 1)]
ONE_HOT = 16
NHOT = 2 * TILES // ONE_HOT


def feed_forward(nc, ctx, block, w, z, moments, out_dram, y_rows):

    def sb(name, shape, dt=F32):
        return ctx.enter_context(nc.sbuf_tensor(name, shape, dt))

    def ps(name, shape):
        return ctx.enter_context(nc.psum_tensor(name, shape, F32))

    def sem(name):
        return ctx.enter_context(nc.semaphore(name))

    x1_rows = nc.dram_tensor("x1_rows", [TOK, E], F32, kind="Internal").ap()

    ident = sb("f_ident", [P, P])
    w_r = sb("w_r", [P, EXP])
    fw1 = sb("fw1_sb", [P, FF])
    fw2 = sb("fw2_sb", [P, FC, E])
    fb1 = sb("fb1_sb", [P, FC])
    fb2 = sb("fb2_sb", [P, E])
    w1 = sb("w1_sb", [P, EXP, FF])
    w2 = sb("w2_sb", [P, EXP, FC, E])
    b1 = sb("b1_sb", [P, EXP, FC])
    b2 = sb("b2_sb", [P, EXP])
    order = sb("order", [P, EXP])
    token_f = sb("token_f", [P, 2, TILES, 2])
    token_no = sb("token_no", [P, 2, TILES, 2], BF16)
    upto_f = sb("upto_f", [P, P])
    slot_lo = sb("slot_lo", [P, P])
    slot_hi = sb("slot_hi", [P, SLOT_TILES])
    upto = sb("upto", [P, P], BF16)
    ones = sb("ones_bf", [P, P], BF16)
    rstd = sb("rstd", [P, TILES])
    std = sb("std", [P, TILES])
    x1s = [sb(f"x1s{i}", [P, ST, E]) for i in range(2)]
    xTs = [sb(f"xTs{i}", [P, S]) for i in range(2)]
    x1T = sb("x1T", [P, CHUNKS, S])
    hidden = [sb(f"hidden{i}", [P, FC, S]) for i in range(2)]
    y_fb = sb("y_fb", [P, TILES, E])
    gathered = sb("gathered", [P, SLOT_TILES, E])
    gatheredT = sb("gatheredT", [P, SLOTS])
    r8 = [sb(f"r8_{i}", [P, TILES, EXP]) for i in range(5)]
    zc, cand, oh1, oh2, slot_of = r8
    r8x = sb("r8x", [P, TILES, EXP])
    r1 = [sb(f"r1_{i}", [P, TILES]) for i in range(12)]
    m1, e2, s1, s2, wt1, wt2, free, elig, before, keep, a1, a2 = r1
    sum8 = sb("sum8", [P, TILES])
    den = sb("den", [P, TILES])
    zeros = sb("zeros", [P, TILES])
    elig_b = sb("elig_b", [P, TILES], BF16)
    before_b = sb("before_b", [P, TILES], BF16)
    slot_u = sb("slot_u", [P, TILES], U32)
    part_u = sb("part_u", [P, TILES], U32)
    slot_c = [sb(f"slot_c{i}", [P, TILES]) for i in range(2)]
    hi_c = [sb(f"hi_c{i}", [P, TILES]) for i in range(2)]
    lo_c = [sb(f"lo_c{i}", [P, TILES]) for i in range(2)]
    one_lo = [gathered[:, 2 * ST * i:2 * ST * (i + 1), :].rearrange("p t e -> p (t e)").bitcast(BF16)
              .rearrange("p (j s) -> p j s", j=ONE_HOT) for i in range(2)]
    one_hi = [sb(f"one_hi{i}", [P, ONE_HOT, SLOT_TILES, 3], BF16) for i in range(2)]
    found = sb("found", [P, SLOT_TILES, 3])
    dest = sb("dest", [P, SLOT_TILES])
    tmp20 = sb("tmp20", [P, SLOT_TILES])
    from_row = sb("from_row", [P, SLOT_TILES], U32)
    to_row = sb("to_row", [P, SLOT_TILES], U32)
    y_in = [gathered[:, 2 * ST * i:2 * ST * (i + 1), :].rearrange("p (n t) e -> p n t e", n=2) for i in range(2)]
    acc = sb("acc", [P, ST, E])
    tile_moments2 = sb("tile_moments2", [P, ST, 2])
    eps_col2 = sb("eps_col2", [P, ST, 2])
    stats2 = sb("stats2", [P, ST, 6])
    moments2 = sb("moments2", [P, TILES, 2])

    tr_ps = ps("tr_ps", [P, S])
    logit_ps = ps("logit_ps", [P, TILES, EXP])
    h_ps = ps("h_ps", [P, 4, S])
    y_ps = ps("y_ps", [P, S])
    rank_ps = ps("rank_ps", [P, 512])

    ld = sem("ld")
    consts = sem("consts")
    std_done = sem("std_done")
    v = sem("v")
    x1_ready = sem("x1_ready")
    x1_kept = sem("x1_kept")
    x1_out = [sem("x1_out0"), sem("x1_out1")]
    tr_wr = sem("tr_wr")
    tr_rd = sem("tr_rd")
    xT_kept = sem("xT_kept")
    logits_wr = sem("logits_wr")
    h_wr = sem("h_wr")
    h_rd = sem("h_rd")
    y_wr = sem("y_wr")
    y_rd = sem("y_rd")
    fb_done = sem("fb_done")
    elig_done = sem("elig_done")
    rank_wr = sem("rank_wr")
    hot_done = sem("hot_done")
    hot_used = sem("hot_used")
    rows_done = sem("rows_done")
    gather_in = sem("gather_in")
    scatter_out = sem("scatter_out")
    logit_e = sem("logit_e")
    zc_done = sem("zc_done")
    y_load = [sem("y_load0"), sem("y_load1")]
    acc_done = sem("acc_done")
    y_part = sem("y_part")
    y_used = sem("y_used")
    aggr2_done = sem("aggr2_done")
    var2_done = sem("var2_done")
    std2_done = sem("std2_done")
    out_ready = sem("out_ready")
    out_out = [sem("out_out0"), sem("out_out1")]

    x1_view = x1_rows.rearrange("(c t p) e -> c p t e", p=P, t=ST)
    y_view = y_rows.rearrange("(k c t p) e -> c k p t e", p=P, t=ST, k=2)
    out_view = out_dram.rearrange("b (t p) e -> b p t e", p=P)
    LOADS = 16 * 14

    def chunks(engine, body):
        for k in (0, 1):
            body(k, k)
        with engine.Fori(1, CHUNKS // 2) as i:
            for c in (0, 1):
                body(2 * i + c, c)

    def later(k):
        return not isinstance(k, int) or k >= 2

    @block.sync
    def _(sp):
        for dst, src in ((ident[:, :], w["ident"]), (w_r[:, :], w["Wr"]), (token_f[:, :, :, :], w["token_no"]),
                         (slot_lo[:, :], w["slot_lo"]), (upto_f[:, :], w["upto"]), (slot_hi[:, :], w["slot_hi"]), (order[:, :], w["order"]),
                         (fw1[:, :], w["fw1"]),
                         (fw2[:, :, :], w["fw2"].rearrange("(c p) n -> p c n", p=P)), (fb1[:, :], w["fb1"]),
                         (fb2[:, :], w["fb2"].rearrange("(a n) -> a n", a=1).to_broadcast([P, E])),
                         (w1[:, :, :], w["W1"].rearrange("e p n -> p e n")),
                         (b1[:, :, :], w["b1"]), (b2[:, :], w["b2"])):
            sp.dma_start(dst, src).then_inc(ld, 16)
        sp.dma_start(w2[:, :, :, :].rearrange("p e c n -> p (e c) n"), w["W2"].rearrange("e (c p) n -> p (e c) n", p=P)).then_inc(ld, 16)
        with sp.Fori(0, CHUNKS // 2) as i:
            for c in (0, 1):
                sp.wait_ge(x1_ready, 2 * i + c + 1)
                sp.dma_start(x1_view[2 * i + c], x1s[c][:, :, :]).then_inc(x1_out[c], 16)
        sp.wait_ge(scatter_out, 16 * SLOT_TILES)

        def load_y(k, c):
            if later(k):
                sp.wait_ge(y_used, k - 1)
            for n in range(2):
                sp.dma_start(y_in[c][:, n, :, :], y_view[k, n]).then_inc(y_load[c], 16)

        chunks(sp, load_y)
        with sp.Fori(0, CHUNKS // 2) as i:
            for c in (0, 1):
                sp.wait_ge(out_ready, 2 * i + c + 1)
                sp.dma_start(out_view[2 * i + c], x1s[c][:, :, :]).then_inc(out_out[c], 16)
        for c in (0, 1):
            sp.wait_ge(out_out[c], 8 * CHUNKS)

    @block.gpsimd
    def _(pool):
        nc.gpsimd.memset(ones[:, :], 1.0).then_inc(consts, 1)
        with pool.Fori(0, CHUNKS // 2) as i:
            for c in (0, 1):
                pool.wait_ge(x1_ready, 2 * i + c + 1)
                nc.gpsimd.tensor_copy(z[:, bass.ds((2 * i + c) * ST, ST), :], x1s[c][:, :, :]).then_inc(x1_kept, 1)
                pool.wait_ge(tr_rd, 2 * i + c + 1)
                nc.gpsimd.tensor_copy(x1T[:, bass.ds(2 * i + c, 1), :].rearrange("p a s -> p (a s)"),
                                      xTs[c][:, :]).then_inc(xT_kept, 1)
        pool.wait_ge(ld, LOADS + 16)
        with pool.Fori(0, CHUNKS) as i:
            pool.wait_ge(y_rd, i + 1)
            yb = y_fb[:, bass.ds(i * ST, ST), :]
            nc.gpsimd.tensor_tensor(yb, yb, fb2[:, :].unsqueeze(1).to_broadcast([P, ST, E]), ALU.add
                                    ).then_inc(fb_done, 1)
        pool.wait_ge(rows_done, 1)
        for c in (0, 1):
            pool.wait_ge(x1_out[c], 8 * CHUNKS)
        for t in range(SLOT_TILES):
            pool.indirect_dma_start(out=gathered[:, t, :], out_offset=None, in_=x1_rows,
                                    in_offset=bass.IndirectOffsetOnAxis(ap=from_row[:, t:t + 1], axis=0)
                                    ).then_inc(gather_in, 16)
        for t in range(SLOT_TILES):
            pool.wait_ge(tr_rd, CHUNKS + SLOT_TILES // ST + t // ST + 1)
            pool.indirect_dma_start(out=y_rows, out_offset=bass.IndirectOffsetOnAxis(ap=to_row[:, t:t + 1], axis=0),
                                    in_=gathered[:, t, :], in_offset=None, bounds_check=2 * TOK - 1,
                                    oob_is_err=False).then_inc(scatter_out, 16)

    @block.tensor
    def _(pe):
        pe.wait_ge(ld, LOADS + 16)
        def route(k, c):
            pe.wait_ge(x1_ready, k + 1)
            if not isinstance(k, int) or k > 0:
                pe.wait_ge(tr_rd, k)
            for t in range(ST):
                mm = nc.tensor.transpose(tr_ps[:, t * P:(t + 1) * P], x1s[c][:, t, :], ident[:, :])
            mm.then_inc(tr_wr, 1)
            pe.wait_ge(tr_rd, k + 1)
            for t in range(ST):
                mm = nc.tensor.matmul(logit_ps[:, bass.ds(k * ST + t, 1), :].rearrange("p a e -> p (a e)"),
                                      xTs[c][:, t * P:(t + 1) * P], w_r[:, :], start=True, stop=True)
            mm.then_inc(logits_wr, 1)

        chunks(pe, route)

        def ranks(e):
            pe.wait_ge(elig_done, e + 1)
            nc.tensor.matmul(rank_ps[:, 0:TILES], upto[:, :], elig_b[:, :], start=True, stop=False)
            nc.tensor.matmul(rank_ps[:, 0:TILES], ones[:, :], before_b[:, :], start=False, stop=True).then_inc(rank_wr, 1)

        def hots(n, slot):
            first = isinstance(n, int) and n == 0
            final = isinstance(n, int) and n == NHOT - 1
            c = slot
            pe.wait_ge(hot_done, n + 1)
            for j in range(ONE_HOT):
                mm = nc.tensor.matmul(rank_ps[:, 128:128 + 3 * SLOT_TILES], one_lo[c][:, j, :],
                                      one_hi[c][:, j, :, :].rearrange("p t v -> p (t v)"),
                                      start=(first and j == 0), stop=(final and j == ONE_HOT - 1))
            mm.then_inc(hot_used, 1)


        pe.wait_ge(xT_kept, CHUNKS)

        def layer1(k):
            for f in range(FC):
                if not isinstance(k, int) or k > 0:
                    pe.wait_ge(h_rd, FC * (k - 1) + f + 1)
                nc.tensor.matmul(h_ps[:, f, :], fw1[:, f * P:(f + 1) * P],
                                 x1T[:, bass.ds(k, 1), :].rearrange("p a s -> p (a s)"),
                                 start=True, stop=True).then_inc(h_wr, 1)

        def layer2(k, c):
            pe.wait_ge(h_rd, FC * k + FC)
            if not isinstance(k, int) or k > 0:
                pe.wait_ge(y_rd, k)
            for t in range(ST):
                for f in range(FC):
                    mm = nc.tensor.matmul(y_ps[:, t * P:(t + 1) * P], hidden[c][:, f, t * P:(t + 1) * P], fw2[:, f, :],
                                          start=(f == 0), stop=(f == FC - 1))
            mm.then_inc(y_wr, 1)

        layer1(0)
        for k in (0, 1):
            layer1(k + 1)
            layer2(k, k)
            ranks(k)
        with pe.Fori(1, EXP // 2) as i:
            for c in (0, 1):
                layer1(2 * i + c + 1)
                layer2(2 * i + c, c)
                ranks(2 * i + c)
        for k in (EXP, EXP + 1):
            layer1(k + 1)
            layer2(k, k % 2)
            hots(k - EXP, k % 2)
        with pe.Fori(EXP // 2 + 1, CHUNKS // 2 - 1) as i:
            for c in (0, 1):
                layer1(2 * i + c + 1)
                layer2(2 * i + c, c)
                hots(2 * i + c - EXP, c)
        layer1(CHUNKS - 1)
        layer2(CHUNKS - 2, 0)
        hots(NHOT - 2, 0)
        layer2(CHUNKS - 1, 1)
        hots(NHOT - 1, 1)

        pe.wait_ge(gather_in, 16 * SLOT_TILES)
        for q in range(SLOT_TILES // ST):
            pe.wait_ge(tr_rd, CHUNKS + q)
            for t in range(ST):
                mm = nc.tensor.transpose(tr_ps[:, t * P:(t + 1) * P], gathered[:, q * ST + t, :], ident[:, :])
            mm.then_inc(tr_wr, 1)
        pe.wait_ge(tr_rd, CHUNKS + SLOT_TILES // ST)

        back = 0
        for e in range(EXP + 1):
            if e < EXP:
                for f in range(FC):
                    pe.wait_ge(h_rd, FC * (CHUNKS + e - 1) + f + 1)
                    nc.tensor.matmul(h_ps[:, f, 0:CAP], w1[:, e, f * P:(f + 1) * P], gatheredT[:, e * CAP:(e + 1) * CAP],
                                     start=True, stop=True).then_inc(h_wr, 1)
            if e > 0:
                pe.wait_ge(h_rd, FC * (CHUNKS + e))
                pe.wait_ge(y_rd, CHUNKS + e - 1)
                for f in range(FC):
                    mm = nc.tensor.matmul(y_ps[:, 0:CAP], w2[:, e - 1, f, :], hidden[(e - 1) % 2][:, f, 0:CAP],
                                          start=(f == 0), stop=(f == FC - 1))
                mm.then_inc(y_wr, 1)
            while back < BACK_AFTER[e]:
                last = ((back + 1) * ST * P - 1) // CAP
                pe.wait_ge(y_rd, CHUNKS + last + 1)
                pe.wait_ge(tr_rd, CHUNKS + SLOT_TILES // ST + back)
                for t in range(ST):
                    s0 = (back * ST + t) * P
                    mm = nc.tensor.transpose(tr_ps[:, t * P:(t + 1) * P], gatheredT[:, s0:s0 + P], ident[:, :])
                mm.then_inc(tr_wr, 1)
                back += 1

    @block.scalar
    def _(act):
        nc.scalar.activation(std[:, :], moments[:, :, 1], ACT.Sqrt).then_inc(std_done, 1)

        def keep_xT(k, c):
            act.wait_ge(tr_wr, k + 1)
            if later(k):
                act.wait_ge(xT_kept, k - 1)
                act.wait_ge(logits_wr, k - 1)
            nc.scalar.copy(xTs[c][:, :], tr_ps[:, :]).then_inc(tr_rd, 1)

        chunks(act, keep_xT)

        def gelus(k, c, width, bias):
            for f in range(FC):
                act.wait_ge(h_wr, FC * k + f + 1)
                if f == 0 and later(k):
                    act.wait_ge(y_wr, k - 1)
                nc.scalar.activation(hidden[c][:, f, 0:width], h_ps[:, f, 0:width], ACT.Gelu,
                                     bias=bias[:, f:f + 1]).then_inc(h_rd, 1)

        def keep_y(k):
            act.wait_ge(y_wr, k + 1)
            nc.scalar.copy(y_fb[:, bass.ds(k * ST, ST), :], y_ps[:, :].rearrange("p (t e) -> p t e", t=ST)
                           ).then_inc(y_rd, 1)

        act.wait_ge(ld, LOADS + 16)

        def fallback(k, c):
            gelus(k, c, S, fb1)
            if not isinstance(k, int) or k > 0:
                keep_y(k - 1)

        chunks(act, fallback)
        keep_y(CHUNKS - 1)

        def keep_tr(q, dst):
            act.wait_ge(tr_wr, CHUNKS + q + 1)
            nc.scalar.copy(dst, tr_ps[:, :]).then_inc(tr_rd, 1)

        for q in range(SLOT_TILES // ST):
            keep_tr(q, gatheredT[:, q * ST * P:(q + 1) * ST * P])

        def keep_expert(e):
            act.wait_ge(y_wr, CHUNKS + e + 1)
            nc.scalar.activation(gatheredT[:, e * CAP:(e + 1) * CAP], y_ps[:, 0:CAP], ACT.Identity,
                                 bias=b2[:, e:e + 1]).then_inc(y_rd, 1)

        back = 0
        for e in range(EXP + 1):
            if e < EXP:
                gelus(CHUNKS + e, e % 2, CAP, b1[:, e, :])
            if e > 0:
                keep_expert(e - 1)
            while back < BACK_AFTER[e]:
                q = SLOT_TILES // ST + back
                keep_tr(q, gathered[:, back * ST:(back + 1) * ST, :].rearrange("p t e -> p (t e)"))
                back += 1
        act.wait_ge(zc_done, 1)
        nc.scalar.activation(cand[:, :, :], zc[:, :, :], ACT.Exp).then_inc(logit_e, 1)
        nc.scalar.activation(e2[:, :], e2[:, :], ACT.Exp).then_inc(logit_e, 1)
        act.wait_ge(var2_done, 1)
        nc.scalar.activation(std[:, :], moments2[:, :, 1], ACT.Sqrt).then_inc(std2_done, 1)

    @block.vector
    def _(dve):
        done = [0]

        def step(ins):
            done[0] += 1
            ins.then_inc(v, 1)
            dve.wait_ge(v, done[0])

        def each(col, n=EXP):
            return col.unsqueeze(2).to_broadcast([P, TILES, n])

        vec = nc.vector
        dve.wait_ge(std_done, 1)
        step(vec.reciprocal(rstd[:, :], std[:, :]))
        base = done[0]

        def normalise(k, c, src, mean, ready, first):
            m = mean[:, bass.ds(k * ST, ST), 0:1].to_broadcast([P, ST, E])
            r = rstd[:, bass.ds(k * ST, ST)].unsqueeze(2).to_broadcast([P, ST, E])
            vec.tensor_tensor(x1s[c][:, :, :], src[:, bass.ds(k * ST, ST), :], m, ALU.subtract).then_inc(v, 1)
            dve.wait_ge(v, first + k + 1)
            vec.tensor_tensor(x1s[c][:, :, :], x1s[c][:, :, :], r, ALU.mult).then_inc(ready, 1)

        def norm1(k, c):
            if later(k):
                dve.wait_ge(x1_kept, k - 1)
                dve.wait_ge(x1_out[c], 8 * (k - c))
                dve.wait_ge(tr_wr, k - 1)
            normalise(k, c, z, moments, x1_ready, base)

        chunks(dve, norm1)
        done[0] = base + CHUNKS

        dve.wait_ge(ld, LOADS + 16)
        vec.tensor_copy(upto[:, :], upto_f[:, :])
        step(vec.tensor_copy(token_no[:, :, :, :], token_f[:, :, :, :]))
        vec.memset(eps_col2[:, :, 0:1], 0.0)
        vec.memset(eps_col2[:, :, 1:2], EPS)
        vec.memset(zeros[:, :], 0.0)
        step(vec.memset(free[:, :], 1.0))

        dve.wait_ge(logits_wr, CHUNKS)
        wide = order[:, :].unsqueeze(1).to_broadcast([P, TILES, EXP])
        step(vec.tensor_reduce(m1[:, :], logit_ps[:, :, :], AX.X, ALU.max))
        step(vec.tensor_tensor(zc[:, :, :], logit_ps[:, :, :], each(m1[:, :]), ALU.subtract))
        step(vec.tensor_scalar(zc[:, :, :], zc[:, :, :], -104.0, None, ALU.max))
        step(vec.scalar_tensor_tensor(cand[:, :, :], zc[:, :, :], 0.0, wide, ALU.is_equal, ALU.mult))
        step(vec.tensor_reduce(m1[:, :], cand[:, :, :], AX.X, ALU.max))
        step(vec.tensor_tensor(oh1[:, :, :], cand[:, :, :], each(m1[:, :]), ALU.is_equal))
        step(vec.scalar_tensor_tensor(slot_of[:, :, :], oh1[:, :, :], -1000.0, zc[:, :, :], ALU.mult, ALU.add))
        step(vec.tensor_reduce(e2[:, :], slot_of[:, :, :], AX.X, ALU.max))
        step(vec.tensor_tensor(cand[:, :, :], slot_of[:, :, :], each(e2[:, :]), ALU.is_equal))
        step(vec.tensor_tensor(cand[:, :, :], cand[:, :, :], wide, ALU.mult))
        step(vec.tensor_reduce(m1[:, :], cand[:, :, :], AX.X, ALU.max))
        step(vec.tensor_tensor(oh2[:, :, :], cand[:, :, :], each(m1[:, :]), ALU.is_equal))
        dve.sem_inc(zc_done, 1)

        for e in range(EXP):
            step(vec.tensor_tensor(elig[:, :], oh1[:, :, e], oh2[:, :, e], ALU.add))
            step(vec.tensor_tensor(elig[:, :], elig[:, :], free[:, :], ALU.mult))
            vec.tensor_copy(elig_b[:, :], elig[:, :])
            step(vec.tensor_tensor_scan(before[:, :], elig[:, :], zeros[:, :], 0.0, ALU.add, ALU.add))
            vec.tensor_tensor(before_b[:, :], before[:, :], elig[:, :], ALU.subtract).then_inc(elig_done, 1)
            dve.wait_ge(rank_wr, e + 1)
            step(vec.scalar_tensor_tensor(keep[:, :], rank_ps[:, 0:TILES], float(CAP), elig[:, :], ALU.is_le, ALU.mult))
            vec.scalar_tensor_tensor(slot_of[:, :, e], rank_ps[:, 0:TILES], float(e * CAP), keep[:, :], ALU.add, ALU.mult)
            step(vec.tensor_tensor(elig[:, :], elig[:, :], keep[:, :], ALU.subtract))
            step(vec.tensor_tensor(free[:, :], free[:, :], elig[:, :], ALU.subtract))

        for c, oh in ((0, oh1), (1, oh2)):
            step(vec.tensor_tensor(r8x[:, :, :], slot_of[:, :, :], oh[:, :, :], ALU.mult))
            step(vec.tensor_reduce(slot_c[c][:, :], r8x[:, :, :], AX.X, ALU.add))
            a = (a1, a2)[c]
            step(vec.tensor_scalar(a[:, :], slot_c[c][:, :], 0.0, None, ALU.is_gt))
            step(vec.scalar_tensor_tensor(elig[:, :], a[:, :], -NOWHERE - 1.0, slot_c[c][:, :], ALU.mult, ALU.add))
            step(vec.tensor_scalar(elig[:, :], elig[:, :], NOWHERE, None, ALU.add))
            step(vec.tensor_copy(slot_u[:, :], elig[:, :]))
            step(vec.tensor_scalar(part_u[:, :], slot_u[:, :], P - 1, None, ALU.bitwise_and))
            step(vec.tensor_copy(lo_c[c][:, :], part_u[:, :]))
            step(vec.tensor_scalar(part_u[:, :], slot_u[:, :], P.bit_length() - 1, None, ALU.logical_shift_right))
            step(vec.tensor_copy(hi_c[c][:, :], part_u[:, :]))

        for n in range(NHOT):
            c, t0 = n // (NHOT // 2), n % (NHOT // 2) * ONE_HOT
            ts = slice(t0, t0 + ONE_HOT)
            if n >= 2:
                dve.wait_ge(hot_used, n - 1)
            lo = lo_c[c][:, ts].unsqueeze(2).to_broadcast([P, ONE_HOT, P])
            vec.tensor_tensor(one_lo[n % 2][:, :, :], lo, slot_lo[:, :].unsqueeze(1).to_broadcast([P, ONE_HOT, P]),
                              ALU.is_equal)
            hot = one_hi[n % 2]
            hi = hi_c[c][:, ts].unsqueeze(2).to_broadcast([P, ONE_HOT, SLOT_TILES])
            step(vec.tensor_tensor(hot[:, :, :, 0], hi,
                                   slot_hi[:, :].unsqueeze(1).to_broadcast([P, ONE_HOT, SLOT_TILES]), ALU.is_equal))
            for j in range(2):
                no = token_no[:, c, ts, j:j + 1].to_broadcast([P, ONE_HOT, SLOT_TILES])
                last = vec.tensor_tensor(hot[:, :, :, 1 + j], hot[:, :, :, 0], no, ALU.mult)
            last.then_inc(hot_done, 1)
        dve.wait_ge(hot_used, NHOT)
        step(vec.tensor_copy(found[:, :, :], rank_ps[:, 128:128 + 3 * SLOT_TILES].rearrange("p (t v) -> p t v", v=3)))
        step(vec.scalar_tensor_tensor(dest[:, :], found[:, :, 1], float(P), found[:, :, 2], ALU.mult, ALU.add))
        step(vec.tensor_scalar(tmp20[:, :], dest[:, :], float(TOK), float(-TOK), ALU.is_ge, ALU.mult))
        step(vec.tensor_tensor(tmp20[:, :], tmp20[:, :], dest[:, :], ALU.add))
        step(vec.tensor_copy(from_row[:, :], tmp20[:, :]))
        step(vec.tensor_scalar(tmp20[:, :], found[:, :, 0], float(-4 * TOK), float(4 * TOK), ALU.mult, ALU.add))
        step(vec.tensor_tensor(tmp20[:, :], tmp20[:, :], dest[:, :], ALU.add))
        vec.tensor_copy(to_row[:, :], tmp20[:, :]).then_inc(rows_done, 1)

        step(vec.tensor_scalar(elig[:, :], free[:, :], -1.0, 1.0, ALU.mult, ALU.add))
        dve.wait_ge(x1_kept, CHUNKS)

        def add_fb(k, c):
            dve.wait_ge(fb_done, k + 1)
            for t in range(ST):
                tile = z[:, bass.ds(k * ST + t, 1), :].rearrange("p a e -> p (a e)")
                yt = y_fb[:, bass.ds(k * ST + t, 1), :].rearrange("p a e -> p (a e)")
                last = vec.scalar_tensor_tensor(tile, yt, elig[:, bass.ds(k * ST + t, 1)], tile, ALU.mult, ALU.add)
            last.then_inc(acc_done, 1)

        chunks(dve, add_fb)

        dve.wait_ge(logit_e, 2)
        step(vec.tensor_reduce(sum8[:, :], cand[:, :, :], AX.X, ALU.add))
        step(vec.reciprocal(s1[:, :], sum8[:, :]))
        step(vec.tensor_tensor(s2[:, :], s1[:, :], e2[:, :], ALU.mult))
        step(vec.tensor_tensor(den[:, :], s1[:, :], s2[:, :], ALU.add))
        step(vec.tensor_scalar(den[:, :], den[:, :], 1e-9, None, ALU.max))
        step(vec.reciprocal(den[:, :], den[:, :]))
        step(vec.tensor_tensor(den[:, :], den[:, :], free[:, :], ALU.mult))
        for a, s_ in ((a1, s1), (a2, s2)):
            step(vec.tensor_tensor(s_[:, :], s_[:, :], den[:, :], ALU.mult))
            step(vec.tensor_tensor(a[:, :], a[:, :], s_[:, :], ALU.mult))
        dve.wait_ge(acc_done, CHUNKS)
        base2 = done[0]

        def combine(k, c):
            dve.wait_ge(y_load[c], 16 * (k - c) + 32)
            for n, a in ((0, a1), (1, a2)):
                for t in range(ST):
                    tile = z[:, bass.ds(k * ST + t, 1), :].rearrange("p a e -> p (a e)")
                    src = tile if n == 0 else acc[:, t, :]
                    last = vec.scalar_tensor_tensor(acc[:, t, :], y_in[c][:, n, t, :], a[:, bass.ds(k * ST + t, 1)],
                                                    src, ALU.mult, ALU.add)
                last.then_inc(y_part, 1)
                dve.wait_ge(y_part, 2 * k + n + 1)
            for t in range(ST):
                last = vec.bn_stats(stats2[:, t, :], acc[:, t, :])
            last.then_inc(y_used, 1)
            dve.wait_ge(y_used, k + 1)
            vec.tensor_scalar(z[:, bass.ds(k * ST, ST), :], acc[:, :, :], 1.0, None, ALU.mult)
            for t in range(ST):
                last = vec.bn_aggr(tile_moments2[:, t, :], stats2[:, t, :])
            last.then_inc(aggr2_done, 1)
            dve.wait_ge(aggr2_done, k + 1)
            vec.tensor_tensor(moments2[:, bass.ds(k * ST, ST), :], tile_moments2[:, :, :], eps_col2[:, :, :], ALU.add
                              ).then_inc(v, 1)
            dve.wait_ge(v, base2 + k + 1)

        chunks(dve, combine)
        dve.sem_inc(var2_done, 1)
        dve.wait_ge(std2_done, 1)
        done[0] = base2 + CHUNKS
        step(vec.reciprocal(rstd[:, :], std[:, :]))
        base3 = done[0]

        def norm2(k, c):
            if later(k):
                dve.wait_ge(out_out[c], 8 * (k - c))
            normalise(k, c, z, moments2, out_ready, base3)

        chunks(dve, norm2)


def program(nc, x, w_qkv, w_out, w, out):
    y_rows = nc.dram_tensor("y_rows", [2 * TOK, E], F32, kind="Internal").ap()
    with nc.sbuf_tensor("z", [P, TILES, E], F32) as z, nc.sbuf_tensor("moments", [P, TILES, 2], F32) as moments:
        with ExitStack() as ctx:
            block = ctx.enter_context(nc.Block())
            nc.disable_value_cache = True
            attention(nc, ctx, block, x, w_qkv, w_out, w["ident"], z, moments, y_rows)
            nc.disable_value_cache = False
        with ExitStack() as ctx:
            block = ctx.enter_context(nc.Block())
            feed_forward(nc, ctx, block, w, z, moments, out, y_rows)


_INPUTS = ["L0_attn_x", "L0_attn_w_qkv", "L0_attn_w_out", "L0_ffn_Wr", "L0_ffn_W1", "L0_ffn_W2", "L0_ffn_fw1",
           "L0_ffn_fw2", "L0_ffn_fb2"]


def kernel(**inputs):
    import numpy as np
    import concourse.bacc as bacc
    from concourse.bass_utils import run_bass_kernel_spmd

    arrays = {name: np.ascontiguousarray(inputs[name]) for name in _INPUTS}
    arrays["fb1"] = np.ascontiguousarray(np.asarray(inputs["L0_ffn_fb1"]).reshape(FC, P).T)
    arrays["b1"] = np.ascontiguousarray(np.asarray(inputs["L0_ffn_b1"]).reshape(EXP, FC, P).transpose(2, 0, 1))
    arrays["b2"] = np.ascontiguousarray(np.asarray(inputs["L0_ffn_b2"]).T)
    arrays["ident"] = np.eye(P, dtype=np.float32)
    arrays["upto"] = np.triu(np.ones((P, P), np.float32))
    arrays["order"] = np.tile(np.arange(EXP, 0, -1, dtype=np.float32), (P, 1))
    arrays["slot_lo"] = np.tile(np.arange(P, dtype=np.float32), (P, 1))
    arrays["slot_hi"] = np.tile(np.arange(SLOT_TILES, dtype=np.float32), (P, 1))
    no = np.zeros((P, 2, TILES, 2), np.float32)
    no[:, 0, :, 0] = np.arange(TILES)
    no[:, 1, :, 0] = np.arange(TILES) + TILES
    no[:, :, :, 1] = np.arange(P)[:, None, None]
    arrays["token_no"] = no

    nc = bacc.Bacc("TRN2", target_bir_lowering=False, num_devices=1)
    aps = {name: nc.dram_tensor("in_" + name, a.shape, mybir.dt.from_np(a.dtype), kind="ExternalInput").ap()
           for name, a in arrays.items()}
    out = nc.dram_tensor("out_0", (BATCH, S, E), F32, kind="ExternalOutput").ap()
    w = {name.replace("L0_ffn_", ""): ap for name, ap in aps.items()}
    program(nc, aps["L0_attn_x"], aps["L0_attn_w_qkv"], aps["L0_attn_w_out"], w, out)
    r = run_bass_kernel_spmd(nc, [{"in_" + name: a for name, a in arrays.items()}], core_ids=[0])
    return r.results[0]["out_0"]
```

```python
from contextlib import ExitStack

import concourse.bass as bass
from concourse import mybir

F32 = mybir.dt.float32
BF16 = mybir.dt.bfloat16
U32 = mybir.dt.uint32
ALU = mybir.AluOpType
ACT = mybir.ActivationFunctionType
AX = mybir.AxisListType

P = 128
BATCH, S, E = 16, 512, 128
H = 16
D = E // H
ST = S // P
SCALE = 1.0 / float(D) ** 0.5
PARTS = 3
QK_ROWS = PARTS * PARTS * D
ROWS = QK_ROWS + PARTS
HALF = H // 2
GROUP = 4
NG = H // GROUP
VW = 32
BANKS = 3
TILES_B = H * ST
ORDER = (((0,), (0,)), ((1,), (1, 2)), ((2, 3), (3,)))
UNITS = NG * ST
EPS = 1e-5


def attention(nc, ctx, block, x_dram, wqkv_dram, wout_dram, ident_dram, z, moments):

    def sb(name, shape, dt):
        return ctx.enter_context(nc.sbuf_tensor(name, shape, dt))

    def ps(name, shape):
        return ctx.enter_context(nc.psum_tensor(name, shape, F32))

    def sem(name):
        return ctx.enter_context(nc.semaphore(name))

    parts_dram = nc.dram_tensor("qk_parts", [2, 2, PARTS, D, H, S], BF16, kind="Internal").ap()

    w_qkv = sb("w_qkv", [P, 3 * E], F32)
    w_out = sb("w_out", [P, E], F32)
    ident = sb("ident", [P, P], F32)
    x_stage = [sb(f"x_stage{i}", [P, ST, E], F32) for i in range(2)]
    xT = [sb(f"xT{i}", [P, S], F32) for i in range(2)]
    part = [sb(f"part{i}", [P, PARTS, S], BF16) for i in range(2)]
    rest = [sb(f"rest{i}", [P, S], F32) for i in range(2)]
    q_stack = [sb(f"q_stack{i}", [P, H, S], BF16) for i in range(2)]
    k_stack = [sb(f"k_stack{i}", [P, H, S], BF16) for i in range(2)]
    v_ones = [sb(f"v_ones{i}", [P, ST, H, VW], F32) for i in range(2)]
    neg_max = [sb(f"neg_max{i}", [P, HALF, ST], F32) for i in range(2)]
    max_part = [sb(f"max_part{i}", [HALF * ST, PARTS, P], BF16) for i in range(2)]
    max_rest = [sb(f"max_rest{i}", [HALF * ST, 2, P], F32) for i in range(2)]
    probs = [sb(f"probs{i}", [P, GROUP, S], F32) for i in range(2)]
    out_raw = [sb(f"out_raw{i}", [P, S], F32) for i in range(2)]
    inv_den = sb("inv_den", [P, ST, GROUP], F32)
    out_tok = [sb(f"out_tok{i}", [P, ST, H, D], F32) for i in range(2)]
    tile_stats = sb("tile_stats", [P, ST, 6], F32)
    tile_moments = sb("tile_moments", [P, ST, 2], F32)
    eps_col = sb("eps_col", [P, ST, 2], F32)
    z_stage = sb("z_stage", [P, ST, E], F32)
    outT = sb("outT", [P, S], F32)


    max_ps = ps("max_ps", [P, 3, S])
    exp_ps = ps("exp_ps", [P, 3, S])
    pv_ps = ps("pv_ps", [P, S])
    misc_ps = ps("misc_ps", [P, S])

    load_w = sem("load_w")
    load_x = [sem("load_x0"), sem("load_x1")]
    load_z = sem("load_z")
    ones_set = sem("ones_set")
    scores_a = sem("scores_a")
    max_done = sem("max_done")
    scores_b = sem("scores_b")
    exp_done = sem("exp_done")
    pv_done = sem("pv_done")
    raw_done = sem("raw_done")
    misc_wr = sem("misc_wr")
    misc_rd = sem("misc_rd")
    part1_done = sem("part1_done")
    parts_done = sem("parts_done")
    part2_done = sem("part2_done")
    parts_out = sem("parts_out")
    stack_in = [[sem(f"stack_in{c}{h}") for h in range(2)] for c in range(2)]
    mpart1 = sem("mpart1")
    mpart2 = sem("mpart2")
    mpart3 = sem("mpart3")
    mrow_in = [sem("mrow_in0"), sem("mrow_in1")]
    stats_done = sem("stats_done")
    aggr_done = sem("aggr_done")
    moments_kept = sem("moments_kept")
    z_kept = sem("z_kept")
    inv_done = sem("inv_done")

    x_tok = x_dram.rearrange("b (t p) e -> b p t e", p=P)

    TASK = {0: "max1", 1: "norm3", 2: "xT", 3: "outT", 4: "proj", 5: "norm0", 6: "q", 7: "k", 8: "v",
            9: "norm1", 10: "max0", 13: "norm2"}
    PRO = 8

    def before_bank(n):
        return n - BANKS + 1 if n >= BANKS else n - (TILES_B - 1) % BANKS if n == 0 else n - BANKS

    def has(task, b):
        if b is None:
            return True
        if task in ("norm3", "outT", "proj"):
            return b > 0
        if task in ("xT", "q", "k"):
            return b < BATCH - 2
        if task in ("max0", "v"):
            return b < BATCH - 1
        return True

    def tasks_before(b, known, u):
        n = sum(1 for v in TASK if v < u and has(TASK[v], known))
        if known is None or known >= 1:
            late = 0
            if known is not None and known == BATCH - 1:
                late = 3
            return 12 * b + 5 - late + n
        return PRO + n

    def batches(engine, body):
        for b in (0, 1):
            body(b, b % 2, b)
        with engine.Fori(1, BATCH // 2 - 1) as i:
            for c in (0, 1):
                body(2 * i + c, c, None)
        for b in (BATCH - 2, BATCH - 1):
            body(b, b % 2, b)

    @block.sync
    def _(sp):
        sp.dma_start(w_qkv[:, :], wqkv_dram).then_inc(load_w, 16)
        sp.dma_start(w_out[:, :], wout_dram).then_inc(load_w, 16)
        sp.dma_start(ident[:, :], ident_dram).then_inc(load_w, 16)
        for b in (0, 1):
            sp.dma_start(x_stage[b][:, :, :], x_tok[b]).then_inc(load_x[b], 16)
        for b in range(BATCH):
            sp.dma_start(z[:, ST * b:ST * (b + 1), :], x_tok[b]).then_inc(load_z, 16)

        def parts_to_dram(b, c):
            sp.wait_ge(parts_done, 2 * b + 2)
            for qk in range(2):
                for n in range(PARTS):
                    sp.dma_start(parts_dram[c, qk, n].rearrange("d h s -> h d s"),
                                 part[qk][:, n, :]).then_inc(parts_out, 16)

        def stack_load(b, c, half):
            sp.wait_ge(parts_out, 96 * b + 96)
            hs = slice(half * HALF, (half + 1) * HALF)
            for n in range(PARTS):
                rows = slice(n * PARTS * D, (n + 1) * PARTS * D)
                for r in range(PARTS):
                    sub = slice((n * PARTS + r) * D, (n * PARTS + r + 1) * D)
                    sp.dma_start(q_stack[c][sub, hs, :], parts_dram[c, 0, n, :, hs, :]).then_inc(stack_in[c][half], 16)
                sp.dma_start(k_stack[c][rows, hs, :],
                             parts_dram[c, 1].rearrange("n d h s -> (n d) h s")[:, hs, :]).then_inc(stack_in[c][half], 16)

        def rows(b, c, half):
            sp.wait_ge(mpart3, 2 * b + half + 1)
            for n in range(PARTS):
                sp.dma_start(q_stack[c][QK_ROWS + n:QK_ROWS + n + 1, half * HALF:(half + 1) * HALF, :],
                               max_part[half][:, n, :]).then_inc(mrow_in[half], 16)

        sp.wait_ge(ones_set, 2)
        for b in (0, 1):
            parts_to_dram(b, b)
            stack_load(b, b, 0)
            stack_load(b, b, 1)
        rows(0, 0, 0)

        def body(b, c, known):
            rows(b, c, 1)
            if known is None or known < BATCH - 2:
                sp.dma_start(x_stage[c][:, :, :], x_tok[b + 2]).then_inc(load_x[c], 16)
                parts_to_dram(b + 2, c)
                sp.wait_ge(scores_b, TILES_B * b + TILES_B // 2)
                stack_load(b + 2, c, 0)
            if known is None or known < BATCH - 1:
                rows(b + 1, 1 - c, 0)
            if known is None or known < BATCH - 2:
                sp.wait_ge(scores_b, TILES_B * b + TILES_B)
                stack_load(b + 2, c, 1)

        batches(sp, body)

    @block.gpsimd
    def _(pool):
        for n, tile in enumerate([k_stack[0][64:P, :, :], k_stack[1][64:P, :, :],
                                  v_ones[0][:, :, :, :], v_ones[1][:, :, :, :]]):
            nc.gpsimd.memset(tile, 1.0).then_inc(ones_set, 1)
            pool.wait_ge(ones_set, n + 1)

        def split(b, qk):
            n = 2 * b + qk
            pool.wait_ge(part2_done, n + 1)
            nc.gpsimd.tensor_tensor(part[qk][:, 2, :], rest[qk][:, :], part[qk][:, 1, :],
                                    ALU.subtract).then_inc(parts_done, 1)

        for b in (0, 1):
            for qk in (0, 1):
                split(b, qk)

        def body(b, c, known):
            if known is None or known < BATCH - 2:
                for qk in (0, 1):
                    split(b + 2, qk)

        batches(pool, body)

    @block.tensor
    def _(pe):
        def misc_turn(count):
            pe.wait_ge(misc_rd, count)

        def t_xT(b, c, count):
            if isinstance(b, int):
                pe.wait_ge(load_x[c], 16 * (b // 2) + 16)
            else:
                pe.wait_ge(load_x[c], 8 * (b - c) + 16)
            misc_turn(count)
            for t in range(ST):
                last = nc.tensor.transpose(misc_ps[:, t * P:(t + 1) * P], x_stage[c][:, t, :], ident[:, :])
            last.then_inc(misc_wr, 1)

        def t_qk(b, c, count, qk):
            misc_turn(count)
            nc.tensor.matmul(misc_ps[:, :], w_qkv[:, qk * E:(qk + 1) * E], xT[c][:, :],
                             start=True, stop=True).then_inc(misc_wr, 1)

        def t_v(b, c, count):
            misc_turn(count)
            for t in range(ST):
                last = nc.tensor.matmul(misc_ps[:, t * P:(t + 1) * P], xT[c][:, t * P:(t + 1) * P],
                                        w_qkv[:, 2 * E:3 * E], start=True, stop=True)
            last.then_inc(misc_wr, 1)

        def t_max(b, half, count):
            pe.wait_ge(max_done, 64 * b + 32 * half + 32)
            misc_turn(count)
            nc.tensor.transpose(misc_ps[0:HALF * ST, 0:P], neg_max[half][:, :, :].rearrange("p h t -> p (h t)"),
                                ident[:, :]).then_inc(misc_wr, 1)

        def t_norm(b, g, count):
            pe.wait_ge(raw_done, NG * b + g + 1)
            misc_turn(count)
            for t in range(ST):
                last = nc.tensor.transpose(misc_ps[:, t * P:(t + 1) * P], out_raw[g % 2][:, t * P:(t + 1) * P],
                                           ident[:, :])
            last.then_inc(misc_wr, 1)

        def t_outT(b, c, count):
            misc_turn(count)
            for t in range(ST):
                last = nc.tensor.transpose(misc_ps[:, t * P:(t + 1) * P],
                                           out_tok[c][:, t, :, :].rearrange("p h d -> p (h d)"), ident[:, :])
            last.then_inc(misc_wr, 1)

        def t_proj(b, count):
            misc_turn(count)
            for t in range(ST):
                last = nc.tensor.matmul(misc_ps[:, t * P:(t + 1) * P], outT[:, t * P:(t + 1) * P], w_out[:, :],
                                        start=True, stop=True)
            last.then_inc(misc_wr, 1)

        def score_max(b, c, h, tiles=range(ST)):
            if h % HALF == 0 and 0 in tiles:
                pe.wait_ge(stack_in[c][h // HALF], 96 * (b - c) + 192)
            for t in tiles:
                n = ST * h + t
                if not isinstance(b, int) or b > 0 or n >= BANKS:
                    pe.wait_ge(max_done, TILES_B * b + before_bank(n))
                nc.tensor.matmul(max_ps[:, n % BANKS, :], q_stack[c][0:QK_ROWS, h, t * P:(t + 1) * P],
                                 k_stack[c][0:QK_ROWS, h, :], start=True, stop=True).then_inc(scores_a, 1)

        def score_exp(b, c, u, heads):
            g, t = u // ST, u % ST
            if u % (UNITS // 2) == 0 and 0 in heads:
                pe.wait_ge(mrow_in[u // (UNITS // 2)], 48 * b + 48)
            for j in heads:
                h = g * GROUP + j
                n = GROUP * u + j
                if not isinstance(b, int) or b > 0 or n >= BANKS:
                    pe.wait_ge(exp_done, TILES_B * b + before_bank(n))
                nc.tensor.matmul(exp_ps[:, n % BANKS, :], k_stack[c][0:ROWS, h, t * P:(t + 1) * P],
                                 q_stack[c][0:ROWS, h, :], start=True, stop=True).then_inc(scores_b, 1)

        def pv(b, v_slot, u):
            g, t = u // ST, u % ST
            pe.wait_ge(exp_done, TILES_B * b + GROUP * u + GROUP)
            if t == 0 and (not isinstance(b, int) or (b, g) != (0, 0)):
                pe.wait_ge(raw_done, NG * b + g)
            for j in range(GROUP):
                mm = nc.tensor.matmul(pv_ps[VW * j:VW * (j + 1), :], v_ones[v_slot][:, t, g * GROUP + j, :],
                                      probs[u % 2][:, j, :], start=(t == 0), stop=(t == ST - 1))
            mm.then_inc(pv_done, 1)

        pe.wait_ge(load_w, 48)
        for b in (0, 1):
            n = 4 * b
            t_xT(b, b, n)
            t_qk(b, b, n + 1, 0)
            t_qk(b, b, n + 2, 1)
            if b == 0:
                t_v(b, b, n + 3)
        for h in range(H):
            score_max(0, 0, h)
            if h == 10:
                t_max(0, 0, PRO - 1)

        def body(b, c, known):
            for u in range(UNITS):
                ahead = known is None or known < BATCH - 1
                for tiles, heads in ORDER:
                    score_exp(b, c, u, heads)
                    if ahead:
                        score_max(b + 1, 1 - c, u, tiles)
                count = tasks_before(b, known, u)
                task = TASK.get(u)
                if task is not None and has(task, known):
                    if task == "xT":
                        t_xT(b + 2, c, count)
                    elif task == "q":
                        t_qk(b + 2, c, count, 0)
                    elif task == "k":
                        t_qk(b + 2, c, count, 1)
                    elif task == "v":
                        t_v(b + 1, 1 - c, count)
                    elif task == "max0":
                        t_max(b + 1, 0, count)
                    elif task == "max1":
                        t_max(b, 1, count)
                    elif task == "norm3":
                        t_norm(b - 1, 3, count)
                    elif task == "outT":
                        t_outT(b - 1, 1 - c, count)
                    elif task == "proj":
                        t_proj(b - 1, count)
                    else:
                        t_norm(b, int(task[-1]), count)
                if u > 0:
                    pv(b, c, u - 1)
                elif known is None or known > 0:
                    pv(b - 1, 1 - c, UNITS - 1)

        batches(pe, body)
        end = tasks_before(BATCH - 1, BATCH - 1, UNITS)
        pv(BATCH - 1, 1, UNITS - 1)
        t_norm(BATCH - 1, 3, end)
        t_outT(BATCH - 1, 1, end + 1)
        t_proj(BATCH - 1, end + 2)

    @block.scalar
    def _(act):
        def exps(b, u):
            if not isinstance(b, int) or 16 * b + u >= 2:
                act.wait_ge(pv_done, 16 * b + u - 1)
            for j in range(GROUP):
                n = GROUP * u + j
                act.wait_ge(scores_b, TILES_B * b + n + 1)
                nc.scalar.activation(probs[u % 2][:, j, :], exp_ps[:, n % BANKS, :], ACT.Exp,
                                     scale=SCALE).then_inc(exp_done, 1)

        def e_xT(b, c, count):
            act.wait_ge(misc_wr, count + 1)
            nc.scalar.copy(xT[c][:, :], misc_ps[:, :]).then_inc(misc_rd, 1)

        def e_part1(b, count, qk):
            act.wait_ge(misc_wr, count + 1)
            if not isinstance(b, int) or b >= 1:
                act.wait_ge(parts_out, 96 * b)
            nc.scalar.copy(part[qk][:, 0, :], misc_ps[:, :]).then_inc(part1_done, 1)

        def e_part2(b, count, qk):
            act.wait_ge(misc_rd, count + 1)
            nc.scalar.copy(part[qk][:, 1, :], rest[qk][:, :]).then_inc(part2_done, 1)

        def e_v(b, c, count):
            act.wait_ge(misc_wr, count + 1)
            nc.scalar.copy(v_ones[c][:, :, :, 0:D], misc_ps[:, :].rearrange("p (t h d) -> p t h d", t=ST, h=H)
                           ).then_inc(misc_rd, 1)

        def e_max(b, half, count):
            act.wait_ge(misc_wr, count + 1)
            if not isinstance(b, int) or b >= 1:
                act.wait_ge(mrow_in[half], 48 * b)
            nc.scalar.copy(max_part[half][:, 0, :], misc_ps[0:HALF * ST, 0:P]).then_inc(mpart1, 1)

        def e_outT(b, count):
            act.wait_ge(misc_wr, count + 1)
            nc.scalar.copy(outT[:, :], misc_ps[:, :]).then_inc(misc_rd, 1)

        def e_raw(b, g, count):
            act.wait_ge(pv_done, 16 * b + 4 * g + 4)
            act.wait_ge(misc_wr, count)
            nc.scalar.copy(out_raw[g % 2][:, :], pv_ps[:, :]).then_inc(raw_done, 1)

        act.wait_ge(ones_set, 4)
        for b in (0, 1):
            n = 4 * b
            e_xT(b, b, n)
            e_part1(b, n + 1, 0)
            e_part1(b, n + 2, 1)
            e_part2(b, n + 1, 0)
            e_part2(b, n + 2, 1)
            if b == 0:
                e_v(b, b, n + 3)
        e_max(0, 0, PRO - 1)

        def body(b, c, known):
            for u in range(UNITS):
                exps(b, u)
                count = tasks_before(b, known, u)
                task = TASK.get(u)
                if task is not None and has(task, known):
                    if task == "xT":
                        e_xT(b + 2, c, count)
                    elif task == "q":
                        e_part1(b + 2, count, 0)
                    elif task == "k":
                        e_part1(b + 2, count, 1)
                    elif task == "v":
                        e_v(b + 1, 1 - c, count)
                    elif task == "max0":
                        e_max(b + 1, 0, count)
                    elif task == "max1":
                        e_max(b, 1, count)
                    elif task == "outT":
                        e_outT(b - 1, count)
                if u in (7, 8) and has("q", known):
                    e_part2(b + 2, tasks_before(b, known, u - 1), u - 7)
                if u % ST == 0 and u > 0:
                    e_raw(b, u // ST - 1, tasks_before(b, known, {4: 0, 8: 2, 12: 6}[u]))
                elif u == 0 and (known is None or known > 0):
                    e_raw(b - 1, NG - 1, tasks_before(b, known, 0))

        batches(act, body)
        end = tasks_before(BATCH - 1, BATCH - 1, UNITS)
        e_raw(BATCH - 1, NG - 1, end)
        e_outT(BATCH - 1, end + 1)

    @block.vector
    def _(dve):
        def maxima(b, h):
            for t in range(ST):
                dve.wait_ge(scores_a, 64 * b + 4 * h + t + 1)
                if h % HALF == 0 and t == 0 and (not isinstance(b, int) or b >= 1):
                    dve.wait_ge(mpart1, 2 * b - 1 + h // HALF)
                nc.vector.tensor_reduce(neg_max[h // HALF][:, h % HALF, t:t + 1], max_ps[:, (ST * h + t) % BANKS, :], AX.X, ALU.max,
                                        negate=True).then_inc(max_done, 1)

        def d_rest1(b, qk):
            n = 2 * b + qk
            dve.wait_ge(part1_done, n + 1)
            if not isinstance(b, int) or b >= 1:
                dve.wait_ge(parts_done, n - 1)
            nc.vector.tensor_tensor(rest[qk][:, :], misc_ps[:, :], part[qk][:, 0, :], ALU.subtract
                                    ).then_inc(misc_rd, 1)

        def d_max(b, half, count):
            n = 2 * b + half
            dve.wait_ge(mpart1, n + 1)
            mp, mr = max_part[half], max_rest[half]
            nc.vector.tensor_tensor(mr[:, 0, :], misc_ps[0:HALF * ST, 0:P], mp[:, 0, :], ALU.subtract).then_inc(misc_rd, 1)
            dve.wait_ge(misc_rd, count + 1)
            nc.vector.tensor_copy(mp[:, 1, :], mr[:, 0, :]).then_inc(mpart2, 1)
            dve.wait_ge(mpart2, n + 1)
            nc.vector.tensor_tensor(mp[:, 2, :], mr[:, 0, :], mp[:, 1, :], ALU.subtract).then_inc(mpart3, 1)

        def d_norm(b, c, g, count):
            n = NG * b + g
            dve.wait_ge(misc_wr, count + 1)
            view = misc_ps[:, :].rearrange("p (t j w) -> p t j w", t=ST, w=VW)
            nc.vector.reciprocal(inv_den[:, :, :], view[:, :, :, D]).then_inc(inv_done, 1)
            dve.wait_ge(inv_done, n + 1)
            nc.vector.tensor_tensor(out_tok[c][:, :, g * GROUP:(g + 1) * GROUP, :], view[:, :, :, 0:D],
                                    inv_den[:, :, :].unsqueeze(3).to_broadcast([P, ST, GROUP, D]), ALU.mult
                                    ).then_inc(misc_rd, 1)

        def d_z(b, count):
            dve.wait_ge(misc_wr, count + 1)
            zb = z[:, bass.ds(b * ST, ST), :]
            nc.vector.tensor_tensor(z_stage[:, :, :], zb, misc_ps[:, :].rearrange("p (t e) -> p t e", t=ST), ALU.add
                                    ).then_inc(misc_rd, 1)
            dve.wait_ge(misc_rd, count + 1)
            for t in range(ST):
                last = nc.vector.bn_stats(tile_stats[:, t, :], z_stage[:, t, :])
            last.then_inc(stats_done, 1)
            dve.wait_ge(stats_done, b + 1)
            nc.vector.tensor_scalar(zb, z_stage[:, :, :], 1.0, None, ALU.mult).then_inc(z_kept, 1)
            for t in range(ST):
                last = nc.vector.bn_aggr(tile_moments[:, t, :], tile_stats[:, t, :])
            last.then_inc(aggr_done, 1)
            dve.wait_ge(aggr_done, b + 1)
            nc.vector.tensor_tensor(moments[:, bass.ds(b * ST, ST), :], tile_moments[:, :, :], eps_col[:, :, :],
                                    ALU.add).then_inc(moments_kept, 1)

        nc.vector.memset(eps_col[:, :, 0:1], 0.0)
        nc.vector.memset(eps_col[:, :, 1:2], EPS)
        for b in (0, 1):
            for qk in (0, 1):
                d_rest1(b, qk)
        for h in range(H):
            maxima(0, h)
            if h == 10:
                d_max(0, 0, PRO - 1)
        dve.wait_ge(load_z, 16 * BATCH)

        def body(b, c, known):
            for u in range(UNITS):
                if known is None or known < BATCH - 1:
                    maxima(b + 1, u)
                count = tasks_before(b, known, u)
                task = TASK.get(u)
                if task is not None and has(task, known):
                    if task == "q":
                        d_rest1(b + 2, 0)
                    elif task == "k":
                        d_rest1(b + 2, 1)
                    elif task == "max0":
                        d_max(b + 1, 0, count)
                    elif task == "max1":
                        d_max(b, 1, count)
                    elif task == "norm3":
                        d_norm(b - 1, 1 - c, 3, count)
                    elif task == "proj":
                        d_z(b - 1, count)
                    elif task.startswith("norm"):
                        d_norm(b, c, int(task[-1]), count)

        batches(dve, body)
        end = tasks_before(BATCH - 1, BATCH - 1, UNITS)
        d_norm(BATCH - 1, 1, 3, end)
        d_z(BATCH - 1, end + 2)


TILES = BATCH * S // P
CHUNKS = BATCH
WAYS = 4
GROUPS = CHUNKS // WAYS
TOK = BATCH * S
FF, EXP, CAP = 512, 8, 320
FC = FF // P
ET = -(-CAP // P)
ET_ROWS = [min(P, CAP - t * P) for t in range(ET)]
FULL = CAP // P
SLOT_TILES = EXP * ET
NOWHERE = 4096.0
ONE_HOT = 16
NHOT = 2 * TILES // ONE_HOT
NV = 6
RANKED = EXP // 2
HOT0 = RANKED + 2
AHEAD = 4


def feed_forward(nc, ctx, block, w, z, moments, out_dram):

    def sb(name, shape, dt=F32):
        return ctx.enter_context(nc.sbuf_tensor(name, shape, dt))

    def ps(name, shape):
        return ctx.enter_context(nc.psum_tensor(name, shape, F32))

    def sem(name):
        return ctx.enter_context(nc.semaphore(name))

    x1_rows = nc.dram_tensor("x1_rows", [TOK, E], F32, kind="Internal").ap()
    sum_rows = nc.dram_tensor("sum_rows", [TOK + ET * P, E], F32, kind="Internal").ap()

    ident = sb("f_ident", [P, P])
    w_r = sb("w_r", [P, VW])
    fw1 = sb("fw1_sb", [P, FF])
    fw2 = sb("fw2_sb", [P, FC, E])
    fb1 = sb("fb1_sb", [P, FC])
    fb2 = sb("fb2_sb", [P, E])
    w1 = sb("w1_sb", [P, EXP, FF])
    w2 = sb("w2_sb", [P, EXP, FC, E])
    b1 = sb("b1_sb", [P, EXP, FC])
    b2 = sb("b2_sb", [P, EXP, E])
    order = sb("order", [P, EXP])
    token_f = sb("token_f", [P, TILES, 2])
    upto_f = sb("upto_f", [P, P])
    slot_lo = sb("slot_lo", [P, P])
    slot_hi = sb("slot_hi", [P, SLOT_TILES])
    spare = sb("spare", [P, SLOT_TILES])
    upto = sb("upto", [P, P], BF16)
    ones = sb("ones_bf", [P, P], BF16)
    zero = sb("f_zero", [P, E])
    rstd = sb("rstd", [P, TILES])
    std = sb("std", [P, TILES])
    x1s = [sb(f"x1s{i}", [P, ST, E]) for i in range(2)]
    x1T = sb("x1T", [P, CHUNKS, S])
    hidden = [sb(f"hidden{i}", [P, FC, S]) for i in range(2)]
    y_fb = sb("y_fb", [P, TILES, E])
    gathered = sb("gathered", [P, SLOT_TILES, E])
    gatheredT = sb("gatheredT", [P, SLOT_TILES, P])
    logits = sb("logits", [P, TILES, EXP])
    r8 = [sb(f"r8_{i}", [P, TILES, EXP]) for i in range(4)]
    zc, oh1, oh2, slot_of = r8
    cand = logits
    r1 = [sb(f"r1_{i}", [P, TILES]) for i in range(12)]
    m1, e2, s1, s2, sum8, den, free, elig, before, keep, a1, a2 = r1
    zeros = sb("zeros", [P, TILES])
    over = sb("over", [P, TILES])
    elig_b = sb("elig_b", [P, TILES], BF16)
    before_b = sb("before_b", [P, TILES], BF16)
    slot_u = sb("slot_u", [P, TILES], U32)
    part_u = sb("part_u", [P, TILES], U32)
    slot_c = sb("slot_c", [P, TILES])
    hi_c = [sb(f"hi_c{i}", [P, TILES]) for i in range(2)]
    lo_c = [sb(f"lo_c{i}", [P, TILES]) for i in range(2)]
    learn = [sb(f"learn{i}", [P, TILES, NV - 1], BF16) for i in range(2)]
    flat = gathered[:, :, :].rearrange("p t e -> p (t e)").bitcast(BF16)
    one_lo = [flat[:, ONE_HOT * P * i:ONE_HOT * P * (i + 1)].rearrange("p (j s) -> p j s", j=ONE_HOT) for i in range(2)]
    flat = gatheredT[:, :, :].rearrange("p t e -> p (t e)").bitcast(BF16)
    hot_w = ONE_HOT * SLOT_TILES * NV
    one_hi = [flat[:, hot_w * i:hot_w * (i + 1)].rearrange("p (j s v) -> p j s v", j=ONE_HOT, v=NV) for i in range(2)]
    logitT = gathered[:, 0:ST, :].rearrange("p t e -> p (t e)")
    found = sb("found", [P, SLOT_TILES, NV])
    dest = sb("dest", [P, SLOT_TILES])
    slot_w = sb("slot_w", [P, SLOT_TILES])
    tmp_s = sb("tmp_s", [P, SLOT_TILES])
    from_row = sb("from_row", [P, SLOT_TILES], U32)
    to_row = sb("to_row", [P, SLOT_TILES], U32)
    sum_in = [y_fb[:, ST * i:ST * (i + 1), :] for i in range(WAYS)]
    out_sb = [y_fb[:, ST * (WAYS + i):ST * (WAYS + i + 1), :] for i in range(WAYS)]
    stats2 = [sb(f"stats2_{i}", [P, ST, 6]) for i in range(WAYS)]
    mv2 = [sb(f"mv2_{i}", [P, ST, 2]) for i in range(WAYS)]
    std2 = [sb(f"std2_{i}", [P, ST]) for i in range(WAYS)]
    rstd2 = [sb(f"rstd2_{i}", [P, ST]) for i in range(WAYS)]
    shift2 = [sb(f"shift2_{i}", [P, ST]) for i in range(WAYS)]
    eps_col = sb("f_eps", [P, 1])

    tr_ps = ps("tr_ps", [P, S])
    logit_ps = ps("logit_ps", [P, S])
    h_ps = ps("h_ps", [P, FC, S])
    y_ps = ps("y_ps", [P, S])
    rank_ps = ps("rank_ps", [P, S])
    hot_ps = rank_ps[:, P:P + NV * SLOT_TILES]
    tr_a = [tr_ps, rank_ps]
    tr_b = [tr_ps, logit_ps]
    y_e = [y_ps, rank_ps]

    ld_route = sem("ld_route")
    ld_fb = sem("ld_fb")
    ld_const = sem("ld_const")
    ld_exp = sem("ld_exp")
    consts = sem("consts")
    std_done = sem("std_done")
    v = sem("v")
    x1_ready = sem("x1_ready")
    x1_kept = sem("x1_kept")
    x1_out = sem("x1_out")
    tr_wr = sem("tr_wr")
    tr_rd = sem("tr_rd")
    lt_wr = sem("lt_wr")
    lt_kept = sem("lt_kept")
    lg_wr = sem("lg_wr")
    lg_kept = sem("lg_kept")
    h_wr = sem("h_wr")
    h_rd = sem("h_rd")
    y_wr = sem("y_wr")
    y_rd = sem("y_rd")
    fb_done = sem("fb_done")
    elig_done = sem("elig_done")
    rank_wr = sem("rank_wr")
    hot_done = sem("hot_done")
    hot_used = sem("hot_used")
    rows_done = sem("rows_done")
    gather_in = [sem(f"gather_in{e}") for e in range(EXP)]
    zc_done = sem("zc_done")
    logit_e = sem("logit_e")
    sum_ready = sem("sum_ready")
    sum_out = sem("sum_out")
    spare_out = sem("spare_out")
    weighed = sem("weighed")
    scatter_out = sem("scatter_out")
    sum_load = [sem(f"sum_load{i}") for i in range(WAYS)]
    stats2_done = sem("stats2_done")
    aggr2_done = sem("aggr2_done")
    std2_done = sem("std2_done")
    rstd2_done = sem("rstd2_done")
    shift2_done = sem("shift2_done")
    out_ready = sem("out_ready")
    out_out = [sem(f"out_out{i}") for i in range(WAYS)]

    def by_chunk(rows):
        return rows.rearrange("(c t p) e -> c p t e", p=P, t=ST)

    x1_view, sum_view = by_chunk(x1_rows), by_chunk(sum_rows[0:TOK, :])
    out_view = out_dram.rearrange("b (t p) e -> b p t e", p=P)
    N_ROUTE, N_FB, N_CONST, N_EXP = 2 * 16, 4 * 16, 6 * 16, 4 * 16

    def groups(engine, body):
        body(0, 0)
        body(1, 1)
        with engine.Fori(2, GROUPS) as g:
            body(g, None)

    def chunk_tiles(k):
        return bass.ds(k * ST, ST)

    @block.sync
    def _(sp):
        sp.wait_ge(consts, 2)
        for dst, src in ((ident[:, :], w["ident"]), (w_r[:, 0:EXP], w["Wr"])):
            sp.dma_start(dst, src).then_inc(ld_route, 16)
        for dst, src in ((fw1[:, :], w["fw1"]), (fb1[:, :], w["fb1"]),
                         (fw2[:, :, :], w["fw2"].rearrange("(c p) n -> p c n", p=P)),
                         (fb2[:, :], w["fb2"].rearrange("(a n) -> a n", a=1).to_broadcast([P, E]))):
            sp.dma_start(dst, src).then_inc(ld_fb, 16)
        for dst, src in ((order[:, :], w["order"]), (upto_f[:, :], w["upto"]), (token_f[:, :, :], w["token_no"]),
                         (slot_lo[:, :], w["slot_lo"]), (slot_hi[:, :], w["slot_hi"]), (spare[:, :], w["spare"])):
            sp.dma_start(dst, src).then_inc(ld_const, 16)
        with sp.Fori(0, CHUNKS) as k:
            sp.wait_ge(x1_kept, k + 1)
            sp.dma_start(x1_view[k], z[:, chunk_tiles(k), :]).then_inc(x1_out, 16)
        sp.wait_ge(consts, 3)
        for t in range(ET):
            sp.dma_start(sum_rows[TOK + t * P:TOK + (t + 1) * P, :], zero[:, :]).then_inc(spare_out, 16)
        for dst, src in ((w1[:, :, :], w["W1"].rearrange("e p n -> p e n")), (b1[:, :, :], w["b1"]),
                         (w2[:, :, :, :].rearrange("p e c n -> p (e c) n"),
                          w["W2"].rearrange("e (c p) n -> p (e c) n", p=P)),
                         (b2[:, :, :].rearrange("p e n -> p (e n)"),
                          w["b2"].rearrange("(a e) n -> a (e n)", a=1).to_broadcast([P, EXP * E]))):
            sp.dma_start(dst, src).then_inc(ld_exp, 16)
        with sp.Fori(0, CHUNKS) as k:
            sp.wait_ge(sum_ready, k + 1)
            sp.dma_start(sum_view[k], z[:, chunk_tiles(k), :]).then_inc(sum_out, 16)

        def load(k, c):
            sp.dma_start(sum_in[c], sum_view[k]).then_inc(sum_load[c], 16)

        def store(k, c):
            sp.wait_ge(out_ready, k + 1)
            sp.dma_start(out_view[k], out_sb[c]).then_inc(out_out[c], 16)

        sp.wait_ge(scatter_out, 16 * SLOT_TILES)
        for c in range(WAYS):
            load(c, c)
        with sp.Fori(0, GROUPS - 1) as g:
            for c in range(WAYS):
                store(g * WAYS + c, c)
                load((g + 1) * WAYS + c, c)
        for c in range(WAYS):
            store((GROUPS - 1) * WAYS + c, c)
        for c in range(WAYS):
            sp.wait_ge(out_out[c], 16 * GROUPS)

    @block.gpsimd
    def _(pool):
        nc.gpsimd.memset(w_r[:, :], 0.0).then_inc(consts, 1)
        nc.gpsimd.memset(ones[:, :], 1.0).then_inc(consts, 1)
        nc.gpsimd.memset(zero[:, :], 0.0).then_inc(consts, 1)
        with pool.Fori(0, CHUNKS // 2) as i:
            for c in (0, 1):
                pool.wait_ge(x1_ready, 2 * i + c + 1)
                nc.gpsimd.tensor_copy(z[:, chunk_tiles(2 * i + c), :], x1s[c][:, :, :]).then_inc(x1_kept, 1)

        def add_fb2(k):
            pool.wait_ge(y_rd, k + 1)
            yb = y_fb[:, chunk_tiles(k), :]
            nc.gpsimd.tensor_tensor(yb, yb, fb2[:, :].unsqueeze(1).to_broadcast([P, ST, E]), ALU.add
                                    ).then_inc(fb_done, 1)

        def gather(e):
            for t in range(ET):
                n = ET_ROWS[t]
                s = e * ET + t
                pool.indirect_dma_start(out=gathered[0:n, s, :], out_offset=None, in_=x1_rows,
                                        in_offset=bass.IndirectOffsetOnAxis(ap=from_row[0:n, s:s + 1], axis=0)
                                        ).then_inc(gather_in[e], 16)

        def scatter(e):
            pool.wait_ge(weighed, e + 1)
            if e > 0:
                pool.wait_ge(scatter_out, 16 * ET * e)
            for t in range(ET):
                n = ET_ROWS[t]
                s = e * ET + t
                pool.indirect_dma_start(out=sum_rows, out_offset=bass.IndirectOffsetOnAxis(ap=to_row[0:n, s:s + 1], axis=0),
                                        in_=gathered[0:n, s, :], in_offset=None,
                                        compute_op=ALU.add).then_inc(scatter_out, 16)

        pool.wait_ge(ld_fb, N_FB)
        with pool.Fori(0, HOT0 + NHOT) as k:
            add_fb2(k)
        pool.wait_ge(rows_done, 1)
        pool.wait_ge(x1_out, 16 * CHUNKS)
        for e in range(AHEAD):
            gather(e)
        for k in range(HOT0 + NHOT, CHUNKS):
            add_fb2(k)
        gather(AHEAD)
        pool.wait_ge(sum_out, 16 * CHUNKS)
        pool.wait_ge(spare_out, 16 * ET)
        for e in range(EXP):
            scatter(e)
            if e + AHEAD + 1 < EXP:
                gather(e + AHEAD + 1)

    @block.tensor
    def _(pe):
        pe.wait_ge(ld_route, N_ROUTE)

        def back(g):
            pe.wait_ge(lt_kept, g + 1)
            for t in range(ST):
                mm = nc.tensor.transpose(y_ps[:, t * P:(t + 1) * P], logitT[:, t * P:(t + 1) * P], ident[:, :])
            mm.then_inc(lg_wr, 1)

        def route(g, known):
            for j in range(WAYS):
                k = g * WAYS + j
                pe.wait_ge(x1_ready, k + 1)
                if known != 0 or j >= 2:
                    pe.wait_ge(tr_rd, k - 1)
                for t in range(ST):
                    mm = nc.tensor.transpose(tr_a[j % 2][:, t * P:(t + 1) * P], x1s[j % 2][:, t, :], ident[:, :])
                mm.then_inc(tr_wr, 1)
            if known != 0:
                if g > 1:
                    pe.wait_ge(lg_kept, g - 1)
                back(g - 1)
            pe.wait_ge(tr_rd, g * WAYS + WAYS)
            for j in range(WAYS):
                mm = nc.tensor.matmul(logit_ps[VW * j:VW * (j + 1), :], w_r[:, :],
                                      x1T[:, g * WAYS + j, :], start=True, stop=True)
            mm.then_inc(lt_wr, 1)

        for g in range(GROUPS):
            route(g, g)
        pe.wait_ge(lg_kept, GROUPS - 1)
        back(GROUPS - 1)

        def ranks(e):
            pe.wait_ge(elig_done, e + 1)
            nc.tensor.matmul(rank_ps[:, 0:TILES], upto[:, :], elig_b[:, :], start=True, stop=False)
            nc.tensor.matmul(rank_ps[:, 0:TILES], ones[:, :], before_b[:, :], start=False, stop=True).then_inc(rank_wr, 1)

        def hots(n):
            pe.wait_ge(hot_done, n + 1)
            for j in range(ONE_HOT):
                mm = nc.tensor.matmul(hot_ps, one_lo[n % 2][:, j, :], one_hi[n % 2][:, j, :, :].rearrange("p t v -> p (t v)"),
                                      start=(n == 0 and j == 0), stop=(n == NHOT - 1 and j == ONE_HOT - 1))
            mm.then_inc(hot_used, 1)

        def layer1(k):
            for f in range(FC):
                if not isinstance(k, int) or k > 0:
                    pe.wait_ge(h_rd, FC * (k - 1) + f + 1)
                nc.tensor.matmul(h_ps[:, f, :], fw1[:, f * P:(f + 1) * P],
                                 x1T[:, bass.ds(k, 1), :].rearrange("p a s -> p (a s)"),
                                 start=True, stop=True).then_inc(h_wr, 1)

        def layer2(k):
            pe.wait_ge(h_rd, FC * k + FC)
            if k == 0:
                pe.wait_ge(lg_kept, GROUPS)
            else:
                pe.wait_ge(y_rd, k)
            for t in range(ST):
                for f in range(FC):
                    mm = nc.tensor.matmul(y_ps[:, t * P:(t + 1) * P], hidden[k % 2][:, f, t * P:(t + 1) * P], fw2[:, f, :],
                                          start=(f == 0), stop=(f == FC - 1))
            mm.then_inc(y_wr, 1)

        pe.wait_ge(ld_fb, N_FB)
        pe.wait_ge(consts, 2)
        layer1(0)
        for k in range(CHUNKS):
            if k + 1 < CHUNKS:
                layer1(k + 1)
            if k < RANKED:
                ranks(2 * k)
            layer2(k)
            if k < RANKED:
                ranks(2 * k + 1)
            if HOT0 <= k < HOT0 + NHOT:
                hots(k - HOT0)

        def rows_T(e):
            pe.wait_ge(gather_in[e], 16 * ET)
            if e >= 2:
                pe.wait_ge(tr_rd, CHUNKS + e - 1)
            for t in range(ET):
                n = ET_ROWS[t]
                mm = nc.tensor.transpose(tr_b[e % 2][:, t * P:t * P + n], gathered[0:n, e * ET + t, :], ident[0:n, 0:n])
            mm.then_inc(tr_wr, 1)

        def expert2(e):
            pe.wait_ge(h_rd, FC * (CHUNKS + e) + FC)
            if e >= 2:
                pe.wait_ge(weighed, e - 1)
            elif e == 0:
                pe.wait_ge(y_rd, CHUNKS)
            for t in range(ET):
                n = ET_ROWS[t]
                for f in range(FC):
                    mm = nc.tensor.matmul(y_e[e % 2][0:n, t * P:(t + 1) * P], hidden[e % 2][:, f, t * P:t * P + n],
                                          w2[:, e, f, :], start=(f == 0), stop=(f == FC - 1))
            mm.then_inc(y_wr, 1)

        pe.wait_ge(ld_exp, N_EXP)
        rows_T(0)
        for e in range(EXP):
            if e + 1 < EXP:
                rows_T(e + 1)
            pe.wait_ge(tr_rd, CHUNKS + e + 1)
            for f in range(FC):
                pe.wait_ge(h_rd, FC * (CHUNKS + e - 1) + f + 1)
                nc.tensor.matmul(h_ps[:, f, 0:CAP], w1[:, e, f * P:(f + 1) * P],
                                 gatheredT[:, e * ET:(e + 1) * ET, :].rearrange("p t e -> p (t e)")[:, 0:CAP],
                                 start=True, stop=True).then_inc(h_wr, 1)
            if e > 0:
                expert2(e - 1)
        expert2(EXP - 1)

    @block.scalar
    def _(act):
        nc.scalar.activation(std[:, :], moments[:, :, 1], ACT.Sqrt).then_inc(std_done, 1)

        def keep_logits(g):
            act.wait_ge(lg_wr, g + 1)
            nc.scalar.copy(logits[:, bass.ds(g * WAYS * ST, WAYS * ST), :].rearrange("p (j t) e -> p t j e", t=ST),
                           y_ps[:, :].rearrange("p (t j x) -> p t j x", t=ST, x=VW)[:, :, :, 0:EXP]).then_inc(lg_kept, 1)

        def route(g, known):
            for j in range(WAYS):
                k = g * WAYS + j
                act.wait_ge(tr_wr, k + 1)
                nc.scalar.copy(x1T[:, bass.ds(k, 1), :].rearrange("p a s -> p (a s)"), tr_a[j % 2][:, :]).then_inc(tr_rd, 1)
            if known != 0:
                keep_logits(g - 1)
            act.wait_ge(lt_wr, g + 1)
            nc.scalar.copy(logitT, logit_ps[:, :]).then_inc(lt_kept, 1)

        groups(act, route)
        keep_logits(GROUPS - 1)

        def gelus(k, width, bias):
            for f in range(FC):
                act.wait_ge(h_wr, FC * k + f + 1)
                if f == 0 and k >= 2:
                    act.wait_ge(y_wr, k - 1)
                nc.scalar.activation(hidden[k % 2][:, f, 0:width], h_ps[:, f, 0:width], ACT.Gelu,
                                     bias=bias[:, f:f + 1]).then_inc(h_rd, 1)

        def keep_y(k):
            act.wait_ge(y_wr, k + 1)
            nc.scalar.copy(y_fb[:, chunk_tiles(k), :], y_ps[:, :].rearrange("p (t e) -> p t e", t=ST)
                           ).then_inc(y_rd, 1)

        act.wait_ge(ld_fb, N_FB)
        for k in range(CHUNKS):
            gelus(k, S, fb1)
            if k > 0:
                keep_y(k - 1)
            if k == 2:
                act.wait_ge(zc_done, 1)
                nc.scalar.activation(cand[:, :, :], zc[:, :, :], ACT.Exp).then_inc(logit_e, 1)
                nc.scalar.activation(e2[:, :], e2[:, :], ACT.Exp).then_inc(logit_e, 1)
        keep_y(CHUNKS - 1)

        def keep_T(e):
            act.wait_ge(tr_wr, CHUNKS + e + 1)
            nc.scalar.copy(gatheredT[:, e * ET:(e + 1) * ET, :].rearrange("p t e -> p (t e)")[:, 0:CAP],
                           tr_b[e % 2][:, 0:CAP]).then_inc(tr_rd, 1)

        act.wait_ge(ld_exp, N_EXP)
        keep_T(0)
        for e in range(EXP):
            if e + 1 < EXP:
                keep_T(e + 1)
            gelus(CHUNKS + e, CAP, b1[:, e, :])

        def normalise(k, c, g_stored):
            act.wait_ge(shift2_done, k + 1)
            if not isinstance(g_stored, int) or g_stored > 0:
                act.wait_ge(out_out[c], 16 * g_stored)
            for t in range(ST):
                last = nc.scalar.activation(out_sb[c][:, t, :], sum_in[c][:, t, :], ACT.Identity,
                                            scale=rstd2[c][:, t:t + 1], bias=shift2[c][:, t:t + 1])
            last.then_inc(out_ready, 1)

        def norm2(g, known):
            for c in range(WAYS):
                k = g * WAYS + c
                act.wait_ge(aggr2_done, k + 1)
                nc.scalar.activation(std2[c][:, :], mv2[c][:, :, 1], ACT.Sqrt, bias=eps_col[:, 0:1]).then_inc(std2_done, 1)
                if c > 0:
                    normalise(k - 1, c - 1, g)
                elif known != 0:
                    normalise(k - 1, WAYS - 1, g - 1)

        groups(act, norm2)
        normalise(CHUNKS - 1, WAYS - 1, GROUPS - 1)

    @block.vector
    def _(dve):
        done = [0]

        def step(ins):
            done[0] += 1
            ins.then_inc(v, 1)
            dve.wait_ge(v, done[0])

        def each(col, n=EXP):
            return col.unsqueeze(2).to_broadcast([P, TILES, n])

        vec = nc.vector
        dve.wait_ge(std_done, 1)
        step(vec.reciprocal(rstd[:, :], std[:, :]))

        def norm1(g, known):
            for j in range(WAYS):
                k = g * WAYS + j
                if known != 0 or j >= 2:
                    dve.wait_ge(x1_kept, k - 1)
                    dve.wait_ge(tr_wr, k - 1)
                for t in range(ST):
                    tile = bass.ds(k * ST + t, 1)
                    last = vec.tensor_scalar(x1s[j % 2][:, t, :], z[:, tile, :].rearrange("p a e -> p (a e)"),
                                             moments[:, tile, 0:1].rearrange("p a e -> p (a e)"), rstd[:, tile],
                                             ALU.subtract, ALU.mult)
                last.then_inc(x1_ready, 1)

        groups(dve, norm1)

        dve.wait_ge(ld_const, N_CONST)
        vec.tensor_copy(upto[:, :], upto_f[:, :])
        for c in (0, 1):
            step(vec.tensor_copy(learn[c][:, :, 0:2], token_f[:, :, :]))
        vec.memset(eps_col[:, :], EPS)
        vec.memset(zeros[:, :], 0.0)
        step(vec.memset(free[:, :], 1.0))

        dve.wait_ge(lg_kept, GROUPS)
        wide = order[:, :].unsqueeze(1).to_broadcast([P, TILES, EXP])
        step(vec.tensor_reduce(m1[:, :], logits[:, :, :], AX.X, ALU.max))
        step(vec.tensor_tensor(zc[:, :, :], logits[:, :, :], each(m1[:, :]), ALU.subtract))
        step(vec.tensor_scalar(zc[:, :, :], zc[:, :, :], -104.0, None, ALU.max))
        step(vec.scalar_tensor_tensor(cand[:, :, :], zc[:, :, :], 0.0, wide, ALU.is_equal, ALU.mult))
        step(vec.tensor_reduce(m1[:, :], cand[:, :, :], AX.X, ALU.max))
        step(vec.tensor_tensor(oh1[:, :, :], cand[:, :, :], each(m1[:, :]), ALU.is_equal))
        step(vec.scalar_tensor_tensor(slot_of[:, :, :], oh1[:, :, :], -1000.0, zc[:, :, :], ALU.mult, ALU.add))
        step(vec.tensor_reduce(e2[:, :], slot_of[:, :, :], AX.X, ALU.max))
        step(vec.tensor_tensor(cand[:, :, :], slot_of[:, :, :], each(e2[:, :]), ALU.is_equal))
        step(vec.tensor_tensor(cand[:, :, :], cand[:, :, :], wide, ALU.mult))
        step(vec.tensor_reduce(m1[:, :], cand[:, :, :], AX.X, ALU.max))
        step(vec.tensor_tensor(oh2[:, :, :], cand[:, :, :], each(m1[:, :]), ALU.is_equal))
        dve.sem_inc(zc_done, 1)

        for e in range(EXP):
            step(vec.tensor_tensor(elig[:, :], oh1[:, :, e], oh2[:, :, e], ALU.add))
            step(vec.tensor_tensor(elig[:, :], elig[:, :], free[:, :], ALU.mult))
            vec.tensor_copy(elig_b[:, :], elig[:, :])
            step(vec.tensor_tensor_scan(before[:, :], elig[:, :], zeros[:, :], 0.0, ALU.add, ALU.add))
            vec.tensor_tensor(before_b[:, :], before[:, :], elig[:, :], ALU.subtract).then_inc(elig_done, 1)
            dve.wait_ge(rank_wr, e + 1)
            step(vec.scalar_tensor_tensor(keep[:, :], rank_ps[:, 0:TILES], float(CAP), elig[:, :], ALU.is_le, ALU.mult))
            vec.scalar_tensor_tensor(slot_of[:, :, e], rank_ps[:, 0:TILES], float(e * ET * P), keep[:, :], ALU.add, ALU.mult)
            step(vec.tensor_tensor(elig[:, :], elig[:, :], keep[:, :], ALU.subtract))
            step(vec.tensor_tensor(free[:, :], free[:, :], elig[:, :], ALU.subtract))
        step(vec.tensor_scalar(over[:, :], free[:, :], -1.0, 1.0, ALU.mult, ALU.add))

        dve.wait_ge(logit_e, 2)
        step(vec.tensor_reduce(sum8[:, :], cand[:, :, :], AX.X, ALU.add))
        step(vec.reciprocal(s1[:, :], sum8[:, :]))
        step(vec.tensor_tensor(s2[:, :], s1[:, :], e2[:, :], ALU.mult))
        step(vec.tensor_tensor(den[:, :], s1[:, :], s2[:, :], ALU.add))
        step(vec.tensor_scalar(den[:, :], den[:, :], 1e-9, None, ALU.max))
        step(vec.reciprocal(den[:, :], den[:, :]))
        step(vec.tensor_tensor(den[:, :], den[:, :], free[:, :], ALU.mult))

        for c, (oh, s_) in enumerate(((oh1, s1), (oh2, s2))):
            step(vec.tensor_tensor(s_[:, :], s_[:, :], den[:, :], ALU.mult))
            for i in range(PARTS):
                step(vec.tensor_copy(learn[c][:, :, 2 + i], s_[:, :]))
                if i < PARTS - 1:
                    step(vec.tensor_tensor(s_[:, :], s_[:, :], learn[c][:, :, 2 + i], ALU.subtract))
            step(vec.tensor_tensor(zc[:, :, :], slot_of[:, :, :], oh[:, :, :], ALU.mult))
            step(vec.tensor_reduce(slot_c[:, :], zc[:, :, :], AX.X, ALU.add))
            step(vec.tensor_scalar(elig[:, :], slot_c[:, :], 0.0, None, ALU.is_gt))
            step(vec.scalar_tensor_tensor(elig[:, :], elig[:, :], -NOWHERE - 1.0, slot_c[:, :], ALU.mult, ALU.add))
            step(vec.tensor_scalar(elig[:, :], elig[:, :], NOWHERE, None, ALU.add))
            step(vec.tensor_copy(slot_u[:, :], elig[:, :]))
            step(vec.tensor_scalar(part_u[:, :], slot_u[:, :], P - 1, None, ALU.bitwise_and))
            step(vec.tensor_copy(lo_c[c][:, :], part_u[:, :]))
            step(vec.tensor_scalar(part_u[:, :], slot_u[:, :], P.bit_length() - 1, None, ALU.logical_shift_right))
            step(vec.tensor_copy(hi_c[c][:, :], part_u[:, :]))

        def add_fb(k):
            dve.wait_ge(fb_done, k + 1)
            for t in range(ST):
                tile = z[:, bass.ds(k * ST + t, 1), :].rearrange("p a e -> p (a e)")
                yt = y_fb[:, bass.ds(k * ST + t, 1), :].rearrange("p a e -> p (a e)")
                last = vec.scalar_tensor_tensor(tile, yt, over[:, bass.ds(k * ST + t, 1)], tile, ALU.mult, ALU.add)
            last.then_inc(sum_ready, 1)

        dve.wait_ge(x1_out, 16 * CHUNKS)
        for n in range(NHOT):
            c, t0 = n // (NHOT // 2), n % (NHOT // 2) * ONE_HOT
            ts = slice(t0, t0 + ONE_HOT)
            if n >= 2:
                dve.wait_ge(hot_used, n - 1)
            lo = lo_c[c][:, ts].unsqueeze(2).to_broadcast([P, ONE_HOT, P])
            vec.tensor_tensor(one_lo[n % 2], lo, slot_lo[:, :].unsqueeze(1).to_broadcast([P, ONE_HOT, P]), ALU.is_equal)
            hot = one_hi[n % 2]
            hi = hi_c[c][:, ts].unsqueeze(2).to_broadcast([P, ONE_HOT, SLOT_TILES])
            step(vec.tensor_tensor(hot[:, :, :, 0], hi,
                                   slot_hi[:, :].unsqueeze(1).to_broadcast([P, ONE_HOT, SLOT_TILES]), ALU.is_equal))
            vec.tensor_tensor(hot[:, :, :, 1:NV], hot[:, :, :, 0:1].to_broadcast([P, ONE_HOT, SLOT_TILES, NV - 1]),
                              learn[c][:, ts, :].unsqueeze(2).to_broadcast([P, ONE_HOT, SLOT_TILES, NV - 1]),
                              ALU.mult).then_inc(hot_done, 1)
            add_fb(n)
        dve.wait_ge(hot_used, NHOT)
        step(vec.tensor_copy(found[:, :, :], hot_ps.rearrange("p (t v) -> p t v", v=NV)))
        step(vec.scalar_tensor_tensor(dest[:, :], found[:, :, 1], float(P), found[:, :, 2], ALU.mult, ALU.add))
        vec.tensor_copy(from_row[:, :], dest[:, :])
        step(vec.tensor_tensor(tmp_s[:, :], found[:, :, 0], spare[:, :], ALU.mult))
        step(vec.tensor_tensor(tmp_s[:, :], spare[:, :], tmp_s[:, :], ALU.subtract))
        step(vec.tensor_tensor(tmp_s[:, :], tmp_s[:, :], dest[:, :], ALU.add))
        step(vec.tensor_copy(to_row[:, :], tmp_s[:, :]))
        step(vec.tensor_tensor(slot_w[:, :], found[:, :, 4], found[:, :, 5], ALU.add))
        vec.tensor_tensor(slot_w[:, :], slot_w[:, :], found[:, :, 3], ALU.add).then_inc(rows_done, 1)
        with dve.Fori(NHOT, CHUNKS) as k:
            add_fb(k)

        dve.wait_ge(rows_done, 1)
        dve.wait_ge(ld_exp, N_EXP)
        for e in range(EXP):
            dve.wait_ge(y_wr, CHUNKS + e + 1)
            y = y_e[e % 2][:, :].rearrange("p (t e) -> p t e", e=E)
            vec.tensor_tensor(gathered[:, e * ET:e * ET + FULL, :], y[:, 0:FULL, :],
                              b2[:, e:e + 1, :].to_broadcast([P, FULL, E]), ALU.add)
            n = ET_ROWS[-1]
            step(vec.tensor_tensor(gathered[0:n, e * ET + FULL, :], y[0:n, FULL, :], b2[0:n, e, :], ALU.add))
            for t in range(ET):
                n = ET_ROWS[t]
                s = e * ET + t
                last = vec.tensor_scalar(gathered[0:n, s, :], gathered[0:n, s, :], slot_w[0:n, s:s + 1], None, ALU.mult)
            last.then_inc(weighed, 1)

        def finish(k, c):
            dve.wait_ge(rstd2_done, k + 1)
            vec.scalar_tensor_tensor(shift2[c][:, :], mv2[c][:, :, 0], -1.0, rstd2[c][:, :], ALU.mult, ALU.mult
                                     ).then_inc(shift2_done, 1)

        def invert(k, c):
            dve.wait_ge(std2_done, k + 1)
            vec.reciprocal(rstd2[c][:, :], std2[c][:, :]).then_inc(rstd2_done, 1)

        def norm2(g, known):
            for c in range(WAYS):
                k = g * WAYS + c
                first = known == 0 and c == 0
                dve.wait_ge(sum_load[c], 16 * (g + 1))
                if known != 0:
                    dve.wait_ge(out_ready, k - WAYS + 1)
                for t in range(ST):
                    last = vec.bn_stats(stats2[c][:, t, :], sum_in[c][:, t, :])
                last.then_inc(stats2_done, 1)
                dve.wait_ge(stats2_done, k + 1)
                if not first:
                    invert(k - 1, (c - 1) % WAYS)
                for t in range(ST):
                    last = vec.bn_aggr(mv2[c][:, t, :], stats2[c][:, t, :])
                last.then_inc(aggr2_done, 1)
                if not first:
                    finish(k - 1, (c - 1) % WAYS)

        groups(dve, norm2)
        invert(CHUNKS - 1, WAYS - 1)
        finish(CHUNKS - 1, WAYS - 1)


def program(nc, x, w_qkv, w_out, w, out):
    with nc.sbuf_tensor("z", [P, TILES, E], F32) as z, nc.sbuf_tensor("moments", [P, TILES, 2], F32) as moments:
        with ExitStack() as ctx:
            block = ctx.enter_context(nc.Block())
            nc.disable_value_cache = True
            attention(nc, ctx, block, x, w_qkv, w_out, w["ident"], z, moments)
            nc.disable_value_cache = False
        with ExitStack() as ctx:
            block = ctx.enter_context(nc.Block())
            feed_forward(nc, ctx, block, w, z, moments, out)


_INPUTS = ["L0_attn_x", "L0_attn_w_qkv", "L0_attn_w_out", "L0_ffn_Wr", "L0_ffn_W1", "L0_ffn_W2", "L0_ffn_fw1",
           "L0_ffn_fw2", "L0_ffn_fb2"]


def kernel(**inputs):
    import numpy as np
    import concourse.bacc as bacc
    from concourse.bass_utils import run_bass_kernel_spmd

    arrays = {name: np.ascontiguousarray(inputs[name]) for name in _INPUTS}
    arrays["fb1"] = np.ascontiguousarray(np.asarray(inputs["L0_ffn_fb1"]).reshape(FC, P).T)
    arrays["b1"] = np.ascontiguousarray(np.asarray(inputs["L0_ffn_b1"]).reshape(EXP, FC, P).transpose(2, 0, 1))
    arrays["b2"] = np.ascontiguousarray(inputs["L0_ffn_b2"])
    arrays["ident"] = np.eye(P, dtype=np.float32)
    arrays["upto"] = np.triu(np.ones((P, P), np.float32))
    arrays["order"] = np.tile(np.arange(EXP, 0, -1, dtype=np.float32), (P, 1))
    arrays["slot_lo"] = np.tile(np.arange(P, dtype=np.float32), (P, 1))
    arrays["slot_hi"] = np.tile(np.arange(SLOT_TILES, dtype=np.float32), (P, 1))
    no = np.zeros((P, TILES, 2), np.float32)
    no[:, :, 0] = np.arange(TILES)
    no[:, :, 1] = np.arange(P)[:, None]
    arrays["token_no"] = no
    own = np.arange(SLOT_TILES)[None, :] % ET * P + np.arange(P)[:, None]
    arrays["spare"] = (TOK + own).astype(np.float32)

    nc = bacc.Bacc("TRN2", target_bir_lowering=False, num_devices=1)
    aps = {name: nc.dram_tensor("in_" + name, a.shape, mybir.dt.from_np(a.dtype), kind="ExternalInput").ap()
           for name, a in arrays.items()}
    out = nc.dram_tensor("out_0", (BATCH, S, E), F32, kind="ExternalOutput").ap()
    w = {name.replace("L0_ffn_", ""): ap for name, ap in aps.items()}
    program(nc, aps["L0_attn_x"], aps["L0_attn_w_qkv"], aps["L0_attn_w_out"], w, out)
    r = run_bass_kernel_spmd(nc, [{"in_" + name: a for name, a in arrays.items()}], core_ids=[0])
    return r.results[0]["out_0"]
```

```python
from contextlib import ExitStack

import concourse.bass as bass
from concourse import mybir

F32 = mybir.dt.float32
BF16 = mybir.dt.bfloat16
U32 = mybir.dt.uint32
ALU = mybir.AluOpType
ACT = mybir.ActivationFunctionType
AX = mybir.AxisListType

P = 128
BATCH, S, E = 16, 512, 128
H = 16
D = E // H
ST = S // P
SCALE = 1.0 / float(D) ** 0.5
PARTS = 3
QK_ROWS = PARTS * PARTS * D
ROWS = QK_ROWS + PARTS
HALF = H // 2
GROUP = 4
NG = H // GROUP
VW = 32
LAST = (BATCH - 1) * ST
NORMED = 2
LEAD = 12
BANKS = 3
TILES_B = H * ST
ORDER = (((0,), (0,)), ((1,), (1, 2)), ((2, 3), (3,)))
UNITS = NG * ST
EPS = 1e-5


def attention(nc, ctx, block, x_dram, wqkv_dram, wout_dram, ident, ident_dram, z, moments, std, rstd, w_r, early_loads):

    def sb(name, shape, dt):
        return ctx.enter_context(nc.sbuf_tensor(name, shape, dt))

    def ps(name, shape):
        return ctx.enter_context(nc.psum_tensor(name, shape, F32))

    def sem(name):
        return ctx.enter_context(nc.semaphore(name))

    parts_dram = nc.dram_tensor("qk_parts", [2, 2, PARTS, D, H, S], BF16, kind="Internal").ap()

    w_qkv = sb("w_qkv", [P, 3 * E], F32)
    w_out = sb("w_out", [P, E], F32)
    x_stage = [sb(f"x_stage{i}", [P, ST, E], F32) for i in range(2)]
    xT = [sb(f"xT{i}", [P, S], F32) for i in range(2)]
    part = [sb(f"part{i}", [P, PARTS, S], BF16) for i in range(2)]
    whole = [sb(f"whole{i}", [P, S], F32) for i in range(2)]
    rest = [sb(f"rest{i}", [P, S], F32) for i in range(2)]
    q_stack = [sb(f"q_stack{i}", [P, H, S], BF16) for i in range(2)]
    k_stack = [sb(f"k_stack{i}", [P, H, S], BF16) for i in range(2)]
    v_ones = [sb(f"v_ones{i}", [P, ST, H, VW], F32) for i in range(2)]
    neg_max = [sb(f"neg_max{i}", [P, HALF, ST], F32) for i in range(2)]
    max_part = [sb(f"max_part{i}", [HALF * ST, PARTS, P], BF16) for i in range(2)]
    max_rest = [sb(f"max_rest{i}", [HALF * ST, 2, P], F32) for i in range(2)]
    probs = [sb(f"probs{i}", [P, GROUP, S], F32) for i in range(2)]
    out_raw = [sb(f"out_raw{i}", [P, S], F32) for i in range(2)]
    inv_den = sb("inv_den", [P, ST, GROUP], F32)
    out_tok = [sb(f"out_tok{i}", [P, ST, H, D], F32) for i in range(2)]
    tile_stats = sb("tile_stats", [P, ST, 6], F32)
    tile_moments = sb("tile_moments", [P, ST, 2], F32)
    eps_col = sb("eps_col", [P, ST, 2], F32)
    attn_out = sb("attn_out", [P, ST, E], F32)
    z_stage = sb("z_stage", [P, ST, E], F32)
    outT = sb("outT", [P, S], F32)


    max_ps = ps("max_ps", [P, 3, S])
    exp_ps = ps("exp_ps", [P, 3, S])
    pv_ps = ps("pv_ps", [P, S])
    misc_ps = ps("misc_ps", [P, S])

    load_w = sem("load_w")
    load_x = [sem("load_x0"), sem("load_x1")]
    load_z = [sem("load_z0"), sem("load_z1")]
    k_ones_set = sem("k_ones_set")
    v_ones_set = sem("v_ones_set")
    scores_a = sem("scores_a")
    max_done = sem("max_done")
    scores_b = sem("scores_b")
    exp_done = sem("exp_done")
    pv_done = sem("pv_done")
    raw_done = sem("raw_done")
    misc_wr = sem("misc_wr")
    misc_rd = sem("misc_rd")
    part1_done = sem("part1_done")
    parts_done = sem("parts_done")
    rest_done = sem("rest_done")
    part2_done = sem("part2_done")
    parts_out = sem("parts_out")
    stack_in = [[sem(f"stack_in{c}{h}") for h in range(2)] for c in range(2)]
    mpart1 = sem("mpart1")
    mpart2 = sem("mpart2")
    mpart3 = sem("mpart3")
    mrow_in = [sem("mrow_in0"), sem("mrow_in1")]
    stats_done = sem("stats_done")
    aggr_done = sem("aggr_done")
    moments_kept = sem("moments_kept")
    attn_kept = sem("attn_kept")
    z_staged = sem("z_staged")
    z_kept = sem("z_kept")
    inv_done = sem("inv_done")
    w_r_zero = sem("w_r_zero")
    early_in = sem("early_in")
    std_early = sem("std_early")
    rstd_early = sem("rstd_early")

    x_tok = x_dram.rearrange("b (t p) e -> b p t e", p=P)

    AT = {"xT": 1, "norm3": 2, "outT": 3, "max1": 4, "q": 5, "proj": 6, "k": 7, "norm0": 9, "v": 10,
          "norm1": 11, "max0": 12, "norm2": 14}
    STATS = AT["proj"] + 4
    TASK = {u: task for task, u in AT.items()}
    RAW_AFTER = {0: 0, 1: AT["norm3"] + 1, 2: AT["norm0"] + 1, 3: 0}
    PRO = 8

    def head_for_maxima(b, c, u, known):
        if u < H - LEAD:
            return b, c, u + LEAD
        if known is None or known < BATCH - 1:
            return b + 1, 1 - c, u - (H - LEAD)
        return None

    def before_bank(n):
        return n - BANKS + 1 if n >= BANKS else n - (TILES_B - 1) % BANKS if n == 0 else n - BANKS

    def has(task, b):
        if b is None:
            return True
        if task in ("norm3", "outT", "proj"):
            return b > 0
        if task in ("xT", "q", "k"):
            return b < BATCH - 2
        if task in ("max0", "v"):
            return b < BATCH - 1
        return True

    def tasks_before(b, known, u):
        n = sum(1 for v in TASK if v < u and has(TASK[v], known))
        if known is None or known >= 1:
            late = 0
            if known is not None and known == BATCH - 1:
                late = 3
            return 12 * b + 5 - late + n
        return PRO + n

    def batches(engine, body):
        for b in (0, 1):
            body(b, b % 2, b)
        with engine.Fori(1, BATCH // 2 - 1) as i:
            for c in (0, 1):
                body(2 * i + c, c, None)
        for b in (BATCH - 2, BATCH - 1):
            body(b, b % 2, b)

    @block.sync
    def _(sp):
        sp.dma_start(w_qkv[:, :], wqkv_dram).then_inc(load_w, 16)
        sp.dma_start(w_out[:, :], wout_dram).then_inc(load_w, 16)
        sp.dma_start(ident[:, :], ident_dram).then_inc(load_w, 16)

        def parts_to_dram(b, c):
            for qk in range(2):
                sp.wait_ge(parts_done, 2 * b + qk + 1)
                sp.dma_start(parts_dram[c, qk].rearrange("n d h s -> (d h) n s"),
                             part[qk][:, :, :]).then_inc(parts_out, 16)

        def stack_load(b, c, half):
            sp.wait_ge(parts_out, 32 * b + 32)
            hs = slice(half * HALF, (half + 1) * HALF)
            q_src, k_src = (parts_dram[c, qk].rearrange("n d h s -> n d (h s)")[:, :, hs.start * S:hs.stop * S]
                            for qk in range(2))
            for n in range(PARTS):
                sp.dma_start(q_stack[c][n * PARTS * D:(n + 1) * PARTS * D, hs, :].rearrange("p h s -> p (h s)"),
                             q_src[n].unsqueeze(0).to_broadcast([PARTS, D, HALF * S])).then_inc(stack_in[c][half], 16)
            sp.dma_start(k_stack[c][0:QK_ROWS, hs, :].rearrange("p h s -> p (h s)"),
                         k_src.rearrange("n d s -> (n d) s").unsqueeze(0).to_broadcast([PARTS, PARTS * D, HALF * S])
                         ).then_inc(stack_in[c][half], 16)

        def rows(b, c, half):
            sp.wait_ge(mpart3, 2 * b + half + 1)
            for n in range(PARTS):
                sp.dma_start(q_stack[c][QK_ROWS + n:QK_ROWS + n + 1, half * HALF:(half + 1) * HALF, :],
                               max_part[half][:, n, :]).then_inc(mrow_in[half], 16)

        for b in (0, 1):
            parts_to_dram(b, b)
            sp.wait_ge(k_ones_set, b + 1)
            stack_load(b, b, 0)
            stack_load(b, b, 1)
        rows(0, 0, 0)
        sp.wait_ge(w_r_zero, 1)
        for dst, src in early_loads:
            sp.dma_start(dst, src).then_inc(early_in, 16)

        def body(b, c, known):
            sp.dma_start(z[:, bass.ds(b * ST, ST), :], x_tok[b]).then_inc(load_z[c], 16)
            rows(b, c, 1)
            if known is None or known < BATCH - 2:
                parts_to_dram(b + 2, c)
                sp.wait_ge(scores_b, TILES_B * b + TILES_B // 2)
                stack_load(b + 2, c, 0)
            if known is None or known < BATCH - 1:
                rows(b + 1, 1 - c, 0)
            if known is None or known < BATCH - 2:
                sp.wait_ge(scores_b, TILES_B * b + TILES_B)
                stack_load(b + 2, c, 1)

        batches(sp, body)
        sp.wait_ge(early_in, 16 * len(early_loads))

    @block.gpsimd
    def _(pool):
        for b in (0, 1):
            pool.dma_start(x_stage[b][:, :, :], x_tok[b]).then_inc(load_x[b], 16)
        nc.gpsimd.memset(w_r[:, :], 0.0).then_inc(w_r_zero, 1)
        for b in (0, 1):
            nc.gpsimd.memset(v_ones[b][:, :, :, :], 1.0).then_inc(v_ones_set, 1)

        def split(b, qk):
            n = 2 * b + qk
            pool.wait_ge(part1_done, n + 1)
            if not isinstance(b, int) or b >= 1:
                pool.wait_ge(parts_done, n - 1)
            nc.gpsimd.tensor_tensor(rest[qk][:, :], whole[qk][:, :], part[qk][:, 0, :], ALU.subtract).then_inc(rest_done, 1)

        def split3(b, qk):
            pool.wait_ge(part2_done, 2 * b + qk + 1)
            nc.gpsimd.tensor_tensor(part[qk][:, 2, :], rest[qk][:, :], part[qk][:, 1, :],
                                    ALU.subtract).then_inc(parts_done, 1)

        def sum_z(b, c):
            pool.wait_ge(load_z[c], 8 * (b - c) + 16)
            pool.wait_ge(attn_kept, b + 1)
            if not isinstance(b, int) or b >= 1:
                pool.wait_ge(stats_done, b)
            zb = z[:, bass.ds(b * ST, ST), :]
            nc.gpsimd.tensor_tensor(z_stage[:, :, :], zb, attn_out[:, :, :], ALU.add).then_inc(z_staged, 1)
            pool.wait_ge(z_staged, b + 1)
            nc.gpsimd.tensor_tensor(zb, zb, attn_out[:, :, :], ALU.add).then_inc(z_kept, 1)

        for b in (0, 1):
            for qk in (0, 1):
                split(b, qk)
            for qk in (0, 1):
                split3(b, qk)

        def body(b, c, known):
            if known is None or known < BATCH - 2:
                pool.dma_start(x_stage[c][:, :, :], x_tok[b + 2]).then_inc(load_x[c], 16)
            for qk in (0, 1):
                if known is None or known < BATCH - 2:
                    split(b + 2, qk)
                    split3(b + 2, qk)
                if qk == 0 and (known is None or known > 0):
                    sum_z(b - 1, 1 - c)

        batches(pool, body)
        sum_z(BATCH - 1, 1)

    @block.tensor
    def _(pe):
        def misc_turn(count):
            pe.wait_ge(misc_rd, count)

        def t_xT(b, c, count):
            if isinstance(b, int):
                pe.wait_ge(load_x[c], 16 * (b // 2) + 16)
            else:
                pe.wait_ge(load_x[c], 8 * (b - c) + 16)
            misc_turn(count)
            for t in range(ST):
                last = nc.tensor.transpose(misc_ps[:, t * P:(t + 1) * P], x_stage[c][:, t, :], ident[:, :])
            last.then_inc(misc_wr, 1)

        def t_qk(b, c, count, qk):
            misc_turn(count)
            nc.tensor.matmul(misc_ps[:, :], w_qkv[:, qk * E:(qk + 1) * E], xT[c][:, :],
                             start=True, stop=True).then_inc(misc_wr, 1)

        def t_v(b, c, count):
            misc_turn(count)
            for t in range(ST):
                last = nc.tensor.matmul(misc_ps[:, t * P:(t + 1) * P], xT[c][:, t * P:(t + 1) * P],
                                        w_qkv[:, 2 * E:3 * E], start=True, stop=True)
            last.then_inc(misc_wr, 1)

        def t_max(b, half, count):
            pe.wait_ge(max_done, 64 * b + 32 * half + 32)
            misc_turn(count)
            nc.tensor.transpose(misc_ps[0:HALF * ST, 0:P], neg_max[half][:, :, :].rearrange("p h t -> p (h t)"),
                                ident[:, :]).then_inc(misc_wr, 1)

        def t_norm(b, g, count):
            pe.wait_ge(raw_done, NG * b + g + 1)
            misc_turn(count)
            for t in range(ST):
                last = nc.tensor.transpose(misc_ps[:, t * P:(t + 1) * P], out_raw[g % 2][:, t * P:(t + 1) * P],
                                           ident[:, :])
            last.then_inc(misc_wr, 1)

        def t_outT(b, c, count):
            misc_turn(count)
            for t in range(ST):
                last = nc.tensor.transpose(misc_ps[:, t * P:(t + 1) * P],
                                           out_tok[c][:, t, :, :].rearrange("p h d -> p (h d)"), ident[:, :])
            last.then_inc(misc_wr, 1)

        def t_proj(b, count):
            misc_turn(count)
            for t in range(ST):
                last = nc.tensor.matmul(misc_ps[:, t * P:(t + 1) * P], outT[:, t * P:(t + 1) * P], w_out[:, :],
                                        start=True, stop=True)
            last.then_inc(misc_wr, 1)

        def score_max(b, c, h, tiles=range(ST)):
            if h % HALF == 0 and 0 in tiles:
                pe.wait_ge(stack_in[c][h // HALF], 32 * (b - c) + 64)
            for t in tiles:
                n = ST * h + t
                if not isinstance(b, int) or b > 0 or n >= BANKS:
                    pe.wait_ge(max_done, TILES_B * b + before_bank(n))
                nc.tensor.matmul(max_ps[:, n % BANKS, :], q_stack[c][0:QK_ROWS, h, t * P:(t + 1) * P],
                                 k_stack[c][0:QK_ROWS, h, :], start=True, stop=True).then_inc(scores_a, 1)

        def score_exp(b, c, u, heads):
            g, t = u // ST, u % ST
            if u % (UNITS // 2) == 0 and 0 in heads:
                pe.wait_ge(mrow_in[u // (UNITS // 2)], 48 * b + 48)
            for j in heads:
                h = g * GROUP + j
                n = GROUP * u + j
                if not isinstance(b, int) or b > 0 or n >= BANKS:
                    pe.wait_ge(exp_done, TILES_B * b + before_bank(n))
                nc.tensor.matmul(exp_ps[:, n % BANKS, :], k_stack[c][0:ROWS, h, t * P:(t + 1) * P],
                                 q_stack[c][0:ROWS, h, :], start=True, stop=True).then_inc(scores_b, 1)

        def pv(b, v_slot, u):
            g, t = u // ST, u % ST
            pe.wait_ge(exp_done, TILES_B * b + GROUP * u + GROUP)
            if t == 0 and (not isinstance(b, int) or (b, g) != (0, 0)):
                pe.wait_ge(raw_done, NG * b + g)
            for j in range(GROUP):
                mm = nc.tensor.matmul(pv_ps[VW * j:VW * (j + 1), :], v_ones[v_slot][:, t, g * GROUP + j, :],
                                      probs[u % 2][:, j, :], start=(t == 0), stop=(t == ST - 1))
            mm.then_inc(pv_done, 1)

        pe.wait_ge(load_w, 48)
        for b in (0, 1):
            n = 4 * b
            t_xT(b, b, n)
            t_qk(b, b, n + 1, 0)
            t_qk(b, b, n + 2, 1)
            if b == 0:
                t_v(b, b, n + 3)
        for h in range(LEAD):
            score_max(0, 0, h)
            if h == HALF:
                t_max(0, 0, PRO - 1)

        def body(b, c, known):
            for u in range(UNITS):
                ahead = head_for_maxima(b, c, u, known)
                for tiles, heads in ORDER:
                    score_exp(b, c, u, heads)
                    if ahead is not None:
                        score_max(*ahead, tiles)
                count = tasks_before(b, known, u)
                task = TASK.get(u)
                if task is not None and has(task, known):
                    if task == "xT":
                        t_xT(b + 2, c, count)
                    elif task == "q":
                        t_qk(b + 2, c, count, 0)
                    elif task == "k":
                        t_qk(b + 2, c, count, 1)
                    elif task == "v":
                        t_v(b + 1, 1 - c, count)
                    elif task == "max0":
                        t_max(b + 1, 0, count)
                    elif task == "max1":
                        t_max(b, 1, count)
                    elif task == "norm3":
                        t_norm(b - 1, 3, count)
                    elif task == "outT":
                        t_outT(b - 1, 1 - c, count)
                    elif task == "proj":
                        t_proj(b - 1, count)
                    else:
                        t_norm(b, int(task[-1]), count)
                if u > 0:
                    pv(b, c, u - 1)
                elif known is None or known > 0:
                    pv(b - 1, 1 - c, UNITS - 1)

        batches(pe, body)
        end = tasks_before(BATCH - 1, BATCH - 1, UNITS)
        pv(BATCH - 1, 1, UNITS - 1)
        t_norm(BATCH - 1, 3, end)
        t_outT(BATCH - 1, 1, end + 1)
        t_proj(BATCH - 1, end + 2)

    @block.scalar
    def _(act):
        def exps(b, u, heads):
            if 0 in heads and (not isinstance(b, int) or 16 * b + u >= 2):
                act.wait_ge(pv_done, 16 * b + u - 1)
            for j in heads:
                n = GROUP * u + j
                act.wait_ge(scores_b, TILES_B * b + n + 1)
                nc.scalar.activation(probs[u % 2][:, j, :], exp_ps[:, n % BANKS, :], ACT.Exp,
                                     scale=SCALE).then_inc(exp_done, 1)

        def e_xT(b, c, count):
            act.wait_ge(misc_wr, count + 1)
            nc.scalar.copy(xT[c][:, :], misc_ps[:, :]).then_inc(misc_rd, 1)

        def e_part1(b, count, qk):
            act.wait_ge(misc_wr, count + 1)
            if not isinstance(b, int) or b >= 1:
                act.wait_ge(parts_out, 32 * b)
            nc.scalar.copy(part[qk][:, 0, :], misc_ps[:, :])

        def e_whole(b, qk):
            nc.scalar.copy(whole[qk][:, :], misc_ps[:, :]).then_inc(part1_done, 1)
            act.wait_ge(part1_done, 2 * b + qk + 1)
            act.sem_inc(misc_rd, 1)

        def e_part2(b, qk):
            act.wait_ge(rest_done, 2 * b + qk + 1)
            nc.scalar.copy(part[qk][:, 1, :], rest[qk][:, :]).then_inc(part2_done, 1)

        def e_v(b, c, count):
            act.wait_ge(misc_wr, count + 1)
            nc.scalar.copy(v_ones[c][:, :, :, 0:D], misc_ps[:, :].rearrange("p (t h d) -> p t h d", t=ST, h=H)
                           ).then_inc(misc_rd, 1)

        def e_max(b, half, count):
            act.wait_ge(misc_wr, count + 1)
            if not isinstance(b, int) or b >= 1:
                act.wait_ge(mrow_in[half], 48 * b)
            nc.scalar.copy(max_part[half][:, 0, :], misc_ps[0:HALF * ST, 0:P]).then_inc(mpart1, 1)

        def e_outT(b, count):
            act.wait_ge(misc_wr, count + 1)
            nc.scalar.copy(outT[:, :], misc_ps[:, :]).then_inc(misc_rd, 1)

        def e_z(b, count):
            act.wait_ge(misc_wr, count + 1)
            if not isinstance(b, int) or b >= 1:
                act.wait_ge(z_kept, b)
            nc.scalar.copy(attn_out[:, :, :], misc_ps[:, :].rearrange("p (t e) -> p t e", t=ST)).then_inc(attn_kept, 1)
            act.wait_ge(attn_kept, b + 1)
            act.sem_inc(misc_rd, 1)

        def e_raw(b, g, count):
            act.wait_ge(pv_done, 16 * b + 4 * g + 4)
            act.wait_ge(misc_wr, count)
            nc.scalar.copy(out_raw[g % 2][:, :], pv_ps[:, :]).then_inc(raw_done, 1)

        for b in (0, 1):
            n = 4 * b
            e_xT(b, b, n)
            e_part1(b, n + 1, 0)
            e_whole(b, 0)
            e_part1(b, n + 2, 1)
            e_whole(b, 1)
            e_part2(b, 0)
            e_part2(b, 1)
            if b == 0:
                act.wait_ge(v_ones_set, 2)
                e_v(b, b, n + 3)
        e_max(0, 0, PRO - 1)

        def body(b, c, known):
            for u in range(UNITS):
                exps(b, u, (0,))
                if has("q", known) and u in (AT["q"] + 1, AT["k"] + 1):
                    e_whole(b + 2, 0 if u == AT["q"] + 1 else 1)
                exps(b, u, (1,))
                if has("q", known) and u == AT["q"] + 2:
                    e_part2(b + 2, 0)
                if u % ST == 1 and u > 1:
                    e_raw(b, u // ST - 1, tasks_before(b, known, RAW_AFTER[u // ST - 1]))
                elif u == 1 and (known is None or known > 0):
                    e_raw(b - 1, NG - 1, tasks_before(b, known, RAW_AFTER[NG - 1]))
                exps(b, u, (2, 3))
                count = tasks_before(b, known, u)
                task = TASK.get(u)
                if task is not None and has(task, known):
                    if task == "xT":
                        e_xT(b + 2, c, count)
                    elif task == "q":
                        e_part1(b + 2, count, 0)
                    elif task == "k":
                        e_part1(b + 2, count, 1)
                    elif task == "v":
                        e_v(b + 1, 1 - c, count)
                    elif task == "max0":
                        e_max(b + 1, 0, count)
                    elif task == "max1":
                        e_max(b, 1, count)
                    elif task == "outT":
                        e_outT(b - 1, count)
                    elif task == "proj":
                        e_z(b - 1, count)
                if has("q", known) and u == AT["k"] + 2:
                    e_part2(b + 2, 1)

        batches(act, body)
        end = tasks_before(BATCH - 1, BATCH - 1, UNITS)
        e_raw(BATCH - 1, NG - 1, end)
        act.wait_ge(moments_kept, BATCH - 1)
        nc.scalar.activation(std[:, 0:LAST], moments[:, 0:LAST, 1], ACT.Sqrt).then_inc(std_early, 1)
        e_outT(BATCH - 1, end + 1)
        e_z(BATCH - 1, end + 2)

    @block.vector
    def _(dve):
        def maximum(b, h, t):
            dve.wait_ge(scores_a, 64 * b + 4 * h + t + 1)
            if h % HALF == 0 and t == 0 and (not isinstance(b, int) or b >= 1):
                dve.wait_ge(mpart1, 2 * b - 1 + h // HALF)
            nc.vector.tensor_reduce(neg_max[h // HALF][:, h % HALF, t:t + 1], max_ps[:, (ST * h + t) % BANKS, :], AX.X, ALU.max,
                                    negate=True).then_inc(max_done, 1)

        def max_rest1(b, half):
            n = 2 * b + half
            dve.wait_ge(mpart1, n + 1)
            nc.vector.tensor_tensor(max_rest[half][:, 0, :], misc_ps[0:HALF * ST, 0:P], max_part[half][:, 0, :], ALU.subtract
                                    ).then_inc(misc_rd, 1)

        def max_part2(b, half, count):
            dve.wait_ge(misc_rd, count + 1)
            nc.vector.tensor_copy(max_part[half][:, 1, :], max_rest[half][:, 0, :]).then_inc(mpart2, 1)

        def max_part3(b, half):
            dve.wait_ge(mpart2, 2 * b + half + 1)
            nc.vector.tensor_tensor(max_part[half][:, 2, :], max_rest[half][:, 0, :], max_part[half][:, 1, :], ALU.subtract
                                    ).then_inc(mpart3, 1)

        by_head = misc_ps[:, :].rearrange("p (t j w) -> p t j w", t=ST, w=VW)

        def invert(count):
            dve.wait_ge(misc_wr, count + 1)
            nc.vector.reciprocal(inv_den[:, :, :], by_head[:, :, :, D]).then_inc(inv_done, 1)

        def normalise(b, c, g):
            dve.wait_ge(inv_done, NG * b + g + 1)
            nc.vector.tensor_tensor(out_tok[c][:, :, g * GROUP:(g + 1) * GROUP, :], by_head[:, :, :, 0:D],
                                    inv_den[:, :, :].unsqueeze(3).to_broadcast([P, ST, GROUP, D]), ALU.mult
                                    ).then_inc(misc_rd, 1)

        def stats(b, t):
            if t == 0:
                dve.wait_ge(z_staged, b + 1)
            last = nc.vector.bn_stats(tile_stats[:, t, :], z_stage[:, t, :])
            if t == ST - 1:
                last.then_inc(stats_done, 1)

        def aggregate(t):
            last = nc.vector.bn_aggr(tile_moments[:, t, :], tile_stats[:, t, :])
            if t == ST - 1:
                last.then_inc(aggr_done, 1)

        def keep_moments(b):
            dve.wait_ge(aggr_done, b + 1)
            nc.vector.tensor_tensor(moments[:, bass.ds(b * ST, ST), :], tile_moments[:, :, :], eps_col[:, :, :],
                                    ALU.add).then_inc(moments_kept, 1)

        for b in (0, 1):
            nc.vector.memset(k_stack[b][64:P, :, :], 1.0).then_inc(k_ones_set, 1)
        nc.vector.memset(eps_col[:, :, 0:1], 0.0)
        nc.vector.memset(eps_col[:, :, 1:2], EPS)
        for h in range(LEAD):
            for t in range(ST):
                maximum(0, h, t)
            if h == HALF:
                max_rest1(0, 0)
                max_part2(0, 0, PRO - 1)
                max_part3(0, 0)

        def body(b, c, known):
            for u in range(UNITS):
                count = tasks_before(b, known, u)
                task, before = TASK.get(u), TASK.get(u - 1)
                task = task if task is not None and has(task, known) else ""
                before = before if before is not None and has(before, known) else ""
                done = known is None or known > 0
                if u == STATS + 1 and done:
                    dve.wait_ge(stats_done, b)
                ahead = head_for_maxima(b, c, u, known)
                for t in range(ST):
                    if ahead is not None:
                        maximum(ahead[0], ahead[2], t)
                    if before.startswith("norm") and t == 0:
                        if before == "norm3":
                            normalise(b - 1, 1 - c, 3)
                        else:
                            normalise(b, c, int(before[-1]))
                    if before.startswith("max") and t < 2:
                        mb, half = (b + 1, 0) if before == "max0" else (b, 1)
                        if t == 0:
                            max_part2(mb, half, tasks_before(b, known, u - 1))
                        else:
                            max_part3(mb, half)
                    if u == STATS and done:
                        stats(b - 1, t)
                    if u == STATS + 1 and done:
                        aggregate(t)
                if u == STATS + 2 and done:
                    keep_moments(b - 1)
                if task.startswith("norm"):
                    invert(count)
                elif task == "max0":
                    max_rest1(b + 1, 0)
                elif task == "max1":
                    max_rest1(b, 1)

        batches(dve, body)
        end = tasks_before(BATCH - 1, BATCH - 1, UNITS)
        invert(end)
        normalise(BATCH - 1, 1, NG - 1)
        dve.wait_ge(std_early, 1)
        nc.vector.reciprocal(rstd[:, 0:LAST], std[:, 0:LAST]).then_inc(rstd_early, 1)
        dve.wait_ge(rstd_early, 1)
        for t in range(NORMED * ST):
            nc.vector.tensor_scalar(z[:, t, :], z[:, t, :], moments[:, t, 0:1], rstd[:, t:t + 1], ALU.subtract, ALU.mult)
        for t in range(ST):
            stats(BATCH - 1, t)
        dve.wait_ge(stats_done, BATCH)
        for t in range(ST):
            aggregate(t)
        keep_moments(BATCH - 1)


TILES = BATCH * S // P
CHUNKS = BATCH
WAYS = 4
GROUPS = CHUNKS // WAYS
TOK = BATCH * S
FF, EXP, CAP = 512, 8, 320
FC = FF // P
ET = -(-CAP // P)
ET_ROWS = [min(P, CAP - t * P) for t in range(ET)]
FULL = CAP // P
SLOT_TILES = EXP * ET
NOWHERE = 4096.0
ONE_HOT = 16
NHOT = 2 * TILES // ONE_HOT
NV = 6
EARLY = 12
RANK_AT = [12, 13, 15, 16, 18, 19, 21, 22]
HOT_AT = [28, 29, 31, 32, 34, 35, 37, 38]
BIASED = 5
AHEAD = 6
NORMS = ((0, 4), (4, 8), (8, 12), (12, 14), (14, 16))
LATE_AT = {0: (12, 13, 14), 1: (15,)}
SCALE_AT = {10: 0, 12: 1, 13: 2, 15: 3}
BIAS_AT = {1: (9,), 3: (10, 11)}
HALVES = (0, 1), (2, 3)
NORM_TILES = ST // 2


def feed_forward(nc, ctx, block, w, ident, z, moments, std, rstd, w_r, fw1, fb1, out_dram):

    def sb(name, shape, dt=F32):
        return ctx.enter_context(nc.sbuf_tensor(name, shape, dt))

    def ps(name, shape):
        return ctx.enter_context(nc.psum_tensor(name, shape, F32))

    def sem(name):
        return ctx.enter_context(nc.semaphore(name))

    x1_rows = nc.dram_tensor("x1_rows", [TOK, E], F32, kind="Internal").ap()
    sum_rows = nc.dram_tensor("sum_rows", [TOK + ET * P, E], F32, kind="Internal").ap()

    fw2 = sb("fw2_sb", [P, FC, E])
    fb2 = sb("fb2_sb", [P, E])
    w1 = sb("w1_sb", [P, EXP, FF])
    w2 = sb("w2_sb", [P, EXP, FC, E])
    b1 = sb("b1_sb", [P, EXP, FC])
    b2 = sb("b2_sb", [P, EXP, E])
    order = sb("order", [P, EXP])
    token_f = sb("token_f", [P, TILES, 2])
    upto_f = sb("upto_f", [P, P])
    slot_lo = sb("slot_lo", [P, P])
    slot_hi = sb("slot_hi", [P, SLOT_TILES])
    spare = sb("spare", [P, SLOT_TILES])
    upto = sb("upto", [P, P], BF16)
    ones = sb("ones_bf", [P, P], BF16)
    zero = sb("f_zero", [P, E])
    x1T = sb("x1T", [P, CHUNKS, S])
    hidden = [sb(f"hidden{i}", [P, FC, S]) for i in range(2)]
    y_fb = sb("y_fb", [P, TILES, E])
    gathered = sb("gathered", [P, SLOT_TILES, E])
    gatheredT = sb("gatheredT", [P, SLOT_TILES, P])
    logits = sb("logits", [P, TILES, EXP])
    r8 = [sb(f"r8_{i}", [P, TILES, EXP]) for i in range(4)]
    zc, oh1, oh2, slot_of = r8
    cand = logits
    m1, e2, sum8, den, free, elig, before, keep = (sb(f"r1_{i}", [P, TILES]) for i in range(8))
    zeros = sb("zeros", [P, TILES])
    over = sb("over", [P, TILES])
    elig_b = sb("elig_b", [P, TILES], BF16)
    before_b = sb("before_b", [P, TILES], BF16)
    score, slot_c, taken, hi_c, lo_c = (sb(name, [P, 2, TILES]) for name in ("score", "slot_c", "taken", "hi_c", "lo_c"))
    slot_u, lo_u, hi_u = (sb(name, [P, 2, TILES], U32) for name in ("slot_u", "lo_u", "hi_u"))
    parts = sb("parts", [P, 2, TILES, NV - 1], BF16)
    learn = [parts[:, c] for c in range(2)]
    flat = gathered[:, :, :].rearrange("p t e -> p (t e)").bitcast(BF16)
    one_lo = [flat[:, ONE_HOT * P * i:ONE_HOT * P * (i + 1)].rearrange("p (j s) -> p j s", j=ONE_HOT) for i in range(2)]
    flat = gatheredT[:, :, :].rearrange("p t e -> p (t e)").bitcast(BF16)
    hot_w = ONE_HOT * SLOT_TILES * NV
    one_hi = [flat[:, hot_w * i:hot_w * (i + 1)].rearrange("p (j s v) -> p j s v", j=ONE_HOT, v=NV) for i in range(2)]
    logitT = gathered[:, 0:ST, :].rearrange("p t e -> p (t e)")
    found = sb("found", [P, SLOT_TILES, NV])
    dest = sb("dest", [P, SLOT_TILES])
    slot_w = sb("slot_w", [P, SLOT_TILES])
    tmp_s = sb("tmp_s", [P, SLOT_TILES])
    from_row = sb("from_row", [P, SLOT_TILES], U32)
    to_row = sb("to_row", [P, SLOT_TILES], U32)
    sums, result = z, y_fb
    stats2 = sb("stats2", [P, TILES, 6])
    shift2 = sb("shift2", [P, TILES])
    eps_col = sb("f_eps", [P, 1])

    tr_ps = ps("tr_ps", [P, S])
    logit_ps = ps("logit_ps", [P, S])
    h_ps = ps("h_ps", [P, FC, S])
    y_ps = ps("y_ps", [P, S])
    rank_ps = ps("rank_ps", [P, S])
    hot_ps = rank_ps[:, P:P + NV * SLOT_TILES]
    tr_b = [tr_ps, logit_ps]
    y_e = [y_ps, rank_ps]

    ld_fb = sem("ld_fb")
    ld_const = sem("ld_const")
    ld_exp = sem("ld_exp")
    consts = sem("consts")
    std_done = sem("std_done")
    v = sem("v")
    x1_ready = sem("x1_ready")
    x1_out = sem("x1_out")
    tr_wr = sem("tr_wr")
    tr_rd = sem("tr_rd")
    lt_wr = sem("lt_wr")
    lt_kept = sem("lt_kept")
    lg_wr = sem("lg_wr")
    lg_kept = sem("lg_kept")
    h_wr = sem("h_wr")
    h_rd = sem("h_rd")
    y_wr = sem("y_wr")
    y_rd = sem("y_rd")
    fb_done = sem("fb_done")
    elig_done = sem("elig_done")
    rank_wr = sem("rank_wr")
    hot_done = sem("hot_done")
    hi_done = sem("hi_done")
    hot_w_done = sem("hot_w_done")
    hot_used = sem("hot_used")
    rows_done = sem("rows_done")
    gather_in = [sem(f"gather_in{e}") for e in range(EXP)]
    zc_done = sem("zc_done")
    logit_e = sem("logit_e")
    sum_ready = sem("sum_ready")
    sum_out = sem("sum_out")
    spare_out = sem("spare_out")
    weighed = sem("weighed")
    scatter_out = sem("scatter_out")
    sum_load = [sem(f"sum_load{k}") for k in range(CHUNKS)]
    stats2_done = sem("stats2_done")
    aggr2_done = sem("aggr2_done")
    std2_done = sem("std2_done")
    rstd2_done = sem("rstd2_done")
    shift2_done = sem("shift2_done")
    out_ready = sem("out_ready")
    out_ready2 = sem("out_ready2")
    out_out = sem("out_out")

    def by_chunk(rows):
        return rows.rearrange("(c t p) e -> c p t e", p=P, t=ST)

    def place(k):
        return k if k < EARLY else k + EXP

    x1_view, sum_view = by_chunk(x1_rows), by_chunk(sum_rows[0:TOK, :])
    sums_view = sum_rows[0:TOK, :].rearrange("(c p t) e -> c p t e", p=P, t=ST)
    out_view = out_dram.rearrange("b (p t) e -> b p t e", t=ST)
    late_out_view = out_dram.rearrange("b (t p) e -> b p t e", p=P)
    N_FB, N_CONST, N_EXP = 2 * 16, 6 * 16, 4 * 16

    def chunk_tiles(k):
        return bass.ds(k * ST, ST)

    @block.sync
    def _(sp):
        for dst, src in ((fw2[:, :, :], w["fw2"].rearrange("(c p) n -> p c n", p=P)),
                         (fb2[:, :], w["fb2"].rearrange("(a n) -> a n", a=1).to_broadcast([P, E]))):
            sp.dma_start(dst, src).then_inc(ld_fb, 16)
        for dst, src in ((order[:, :], w["order"]), (upto_f[:, :], w["upto"]), (token_f[:, :, :], w["token_no"]),
                         (slot_lo[:, :], w["slot_lo"]), (slot_hi[:, :], w["slot_hi"]), (spare[:, :], w["spare"])):
            sp.dma_start(dst, src).then_inc(ld_const, 16)
        with sp.Fori(0, CHUNKS) as k:
            sp.wait_ge(x1_ready, k + 1)
            sp.dma_start(x1_view[k], z[:, chunk_tiles(k), :]).then_inc(x1_out, 16)
        for k in range(EARLY, CHUNKS):
            sp.dma_start(sum_view[k], z[:, chunk_tiles(k), :]).then_inc(sum_out, 16)
        sp.wait_ge(consts, 2)
        for t in range(ET):
            sp.dma_start(sum_rows[TOK + t * P:TOK + (t + 1) * P, :], zero[:, :]).then_inc(spare_out, 16)
        for dst, src in ((w1[:, :, :], w["W1"].rearrange("e p n -> p e n")), (b1[:, :, :], w["b1"]),
                         (w2[:, :, :, :].rearrange("p e c n -> p (e c) n"),
                          w["W2"].rearrange("e (c p) n -> p (e c) n", p=P)),
                         (b2[:, :, :].rearrange("p e n -> p (e n)"),
                          w["b2"].rearrange("(a e) n -> a (e n)", a=1).to_broadcast([P, EXP * E]))):
            sp.dma_start(dst, src).then_inc(ld_exp, 16)
        with sp.Fori(0, EARLY) as k:
            sp.wait_ge(sum_ready, k + 1)
            sp.dma_start(sum_view[k], z[:, chunk_tiles(k), :]).then_inc(sum_out, 16)

        sp.wait_ge(scatter_out, 16 * SLOT_TILES)
        for k in range(CHUNKS):
            view = sums_view if k < EARLY else sum_view
            sp.dma_start(sums[:, chunk_tiles(k), :], view[k]).then_inc(sum_load[k], 16)
        for view, chunks in ((out_view, (0, EARLY)), (late_out_view, (EARLY, CHUNKS))):
            with sp.Fori(*chunks) as k:
                sp.wait_ge(out_ready, k + 1)
                sp.wait_ge(out_ready2, k + 1)
                sp.dma_start(view[k], result[:, chunk_tiles(k), :]).then_inc(out_out, 16)
        sp.wait_ge(out_out, 16 * CHUNKS)

    @block.gpsimd
    def _(pool):
        nc.gpsimd.memset(ones[:, :], 1.0).then_inc(consts, 1)
        nc.gpsimd.memset(zero[:, :], 0.0).then_inc(consts, 1)

        def add_fb2(k):
            pool.wait_ge(y_rd, k + 1)
            yb = y_fb[:, chunk_tiles(k), :]
            nc.gpsimd.tensor_tensor(yb, yb, fb2[:, :].unsqueeze(1).to_broadcast([P, ST, E]), ALU.add
                                    ).then_inc(fb_done, 1)

        def gather(e):
            for t in range(ET):
                n = ET_ROWS[t]
                s = e * ET + t
                pool.indirect_dma_start(out=gathered[0:n, s, :], out_offset=None, in_=x1_rows,
                                        in_offset=bass.IndirectOffsetOnAxis(ap=from_row[0:n, s:s + 1], axis=0)
                                        ).then_inc(gather_in[e], 16)

        def scatter(e):
            pool.wait_ge(weighed, e + 1)
            if e > 0:
                pool.wait_ge(scatter_out, 16 * ET * e)
            for t in range(ET):
                n = ET_ROWS[t]
                s = e * ET + t
                pool.indirect_dma_start(out=sum_rows, out_offset=bass.IndirectOffsetOnAxis(ap=to_row[0:n, s:s + 1], axis=0),
                                        in_=gathered[0:n, s, :], in_offset=None,
                                        compute_op=ALU.add).then_inc(scatter_out, 16)

        pool.wait_ge(ld_fb, N_FB)
        with pool.Fori(0, BIASED) as k:
            add_fb2(k)
        for n in range(NHOT):
            c, t0 = n // (NHOT // 2), n % (NHOT // 2) * ONE_HOT
            pool.wait_ge(hi_done, n + 1)
            hot = one_hi[n % 2]
            nc.gpsimd.tensor_tensor(hot[:, :, :, 3:NV], hot[:, :, :, 0:1].to_broadcast([P, ONE_HOT, SLOT_TILES, PARTS]),
                                    learn[c][:, t0:t0 + ONE_HOT, 2:].unsqueeze(2).to_broadcast([P, ONE_HOT, SLOT_TILES, PARTS]),
                                    ALU.mult).then_inc(hot_w_done, 1)
            if n % 2 == 1:
                add_fb2(BIASED + n // 2)
        pool.wait_ge(rows_done, 1)
        pool.wait_ge(x1_out, 16 * CHUNKS)
        for e in range(AHEAD):
            gather(e)
            for k in BIAS_AT.get(e, ()):
                add_fb2(k)
        pool.wait_ge(sum_out, 16 * CHUNKS)
        pool.wait_ge(spare_out, 16 * ET)
        for e in range(EXP):
            scatter(e)
            if e + AHEAD < EXP:
                gather(e + AHEAD)

        for n, (first, end) in enumerate(NORMS):
            for k in LATE_AT.get(n, ()):
                add_fb2(k)
            pool.wait_ge(shift2_done, n + 1)
            for k in range(first, end):
                for tile in range(k * ST + NORM_TILES, (k + 1) * ST):
                    last = nc.gpsimd.tensor_scalar(result[:, tile, :], sums[:, tile, :], rstd[:, tile:tile + 1],
                                                   shift2[:, tile:tile + 1], ALU.mult, ALU.add)
                last.then_inc(out_ready2, 1)

    @block.tensor
    def _(pe):
        def ranks(e):
            pe.wait_ge(elig_done, e + 1)
            nc.tensor.matmul(rank_ps[:, 0:TILES], upto[:, :], elig_b[:, :], start=True, stop=False)
            nc.tensor.matmul(rank_ps[:, 0:TILES], ones[:, :], before_b[:, :], start=False, stop=True).then_inc(rank_wr, 1)

        def hots(n):
            pe.wait_ge(hot_done, n + 1)
            pe.wait_ge(hot_w_done, n + 1)
            for j in range(ONE_HOT):
                mm = nc.tensor.matmul(hot_ps, one_lo[n % 2][:, j, :], one_hi[n % 2][:, j, :, :].rearrange("p t v -> p (t v)"),
                                      start=(n == 0 and j == 0), stop=(n == NHOT - 1 and j == ONE_HOT - 1))
            mm.then_inc(hot_used, 1)

        def layer1(k, tiles):
            for f in tiles:
                if k > 0:
                    pe.wait_ge(h_rd, FC * (place(k) - 1) + f + 1)
                nc.tensor.matmul(h_ps[:, f, :], fw1[:, f * P:(f + 1) * P], x1T[:, k, :],
                                 start=True, stop=True).then_inc(h_wr, 1)

        def layer2(k, tiles):
            if 0 in tiles:
                pe.wait_ge(h_rd, FC * place(k) + FC)
                if k > 0:
                    pe.wait_ge(y_rd, k)
                if k == EARLY:
                    pe.wait_ge(weighed, EXP - 1)
            for t in tiles:
                for f in range(FC):
                    mm = nc.tensor.matmul(y_ps[:, t * P:(t + 1) * P], hidden[place(k) % 2][:, f, t * P:(t + 1) * P], fw2[:, f, :],
                                          start=(f == 0), stop=(f == FC - 1))
            if ST - 1 in tiles:
                mm.then_inc(y_wr, 1)

        def chunk_T(k):
            pe.wait_ge(x1_ready, k + 1)
            if k > 0:
                pe.wait_ge(tr_rd, k)
            for t in range(ST):
                mm = nc.tensor.transpose(tr_ps[:, t * P:(t + 1) * P], z[:, k * ST + t, :], ident[:, :])
            mm.then_inc(tr_wr, 1)

        def router(g):
            pe.wait_ge(tr_rd, g * WAYS + WAYS)
            for j in range(WAYS):
                mm = nc.tensor.matmul(logit_ps[VW * j:VW * (j + 1), :], w_r[:, :], x1T[:, g * WAYS + j, :],
                                      start=True, stop=True)
            mm.then_inc(lt_wr, 1)

        def back(g):
            pe.wait_ge(lt_kept, g + 1)
            if g > 0:
                pe.wait_ge(lg_kept, g)
            for t in range(ST):
                mm = nc.tensor.transpose(rank_ps[:, t * P:(t + 1) * P], logitT[:, t * P:(t + 1) * P], ident[:, :])
            mm.then_inc(lg_wr, 1)

        pieces = [(layer1, 0), (layer1, 1), (layer2, 0), (layer1, 2)]
        for g in range(GROUPS):
            k = g * WAYS
            product, chunk = pieces[g]
            for j in range(WAYS):
                chunk_T(k + j)
                if product is layer2 and j == 0:
                    pe.wait_ge(ld_fb, N_FB)
                if product is layer1 and j == 0:
                    pe.wait_ge(tr_rd, chunk + 1)
                product(chunk, [j])
                if j == 1 and g > 0:
                    back(g - 1)
            router(g)
        for half in (0, 1):
            layer2(1, HALVES[half])
            if half == 0:
                back(GROUPS - 1)

        pe.wait_ge(consts, 1)
        for k in range(2, EARLY):
            for half in range(4):
                step = 4 * k + half
                if half >= 2:
                    layer2(k, HALVES[half - 2])
                elif k + 1 < EARLY:
                    layer1(k + 1, HALVES[half])
                if step in RANK_AT:
                    if step == RANK_AT[0]:
                        pe.wait_ge(lg_kept, GROUPS)
                    ranks(RANK_AT.index(step))
                if step in HOT_AT:
                    hots(HOT_AT.index(step))

        def rows_T(e):
            pe.wait_ge(gather_in[e], 16 * ET)
            if e >= 2:
                pe.wait_ge(tr_rd, CHUNKS + e - 1)
            for t in range(ET):
                n = ET_ROWS[t]
                mm = nc.tensor.transpose(tr_b[e % 2][:, t * P:t * P + n], gathered[0:n, e * ET + t, :], ident[0:n, 0:n])
            mm.then_inc(tr_wr, 1)

        def expert2(e):
            pe.wait_ge(h_rd, FC * (EARLY + e) + FC)
            if e >= 2:
                pe.wait_ge(weighed, e - 1)
            elif e == 0:
                pe.wait_ge(y_rd, EARLY)
            for t in range(ET):
                n = ET_ROWS[t]
                for f in range(FC):
                    mm = nc.tensor.matmul(y_e[e % 2][0:n, t * P:(t + 1) * P], hidden[e % 2][:, f, t * P:t * P + n],
                                          w2[:, e, f, :], start=(f == 0), stop=(f == FC - 1))
            mm.then_inc(y_wr, 1)

        pe.wait_ge(ld_exp, N_EXP)
        rows_T(0)
        for e in range(EXP):
            if e + 1 < EXP:
                rows_T(e + 1)
            pe.wait_ge(tr_rd, CHUNKS + e + 1)
            for f in range(FC):
                pe.wait_ge(h_rd, FC * (EARLY + e - 1) + f + 1)
                nc.tensor.matmul(h_ps[:, f, 0:CAP], w1[:, e, f * P:(f + 1) * P],
                                 gatheredT[:, e * ET:(e + 1) * ET, :].rearrange("p t e -> p (t e)")[:, 0:CAP],
                                 start=True, stop=True).then_inc(h_wr, 1)
            if e > 0:
                expert2(e - 1)
        layer1(EARLY, range(FC))
        expert2(EXP - 1)
        for k in range(EARLY, CHUNKS):
            if k + 1 < CHUNKS:
                layer1(k + 1, range(FC))
            layer2(k, range(ST))

    @block.scalar
    def _(act):
        nc.scalar.activation(std[:, LAST:], moments[:, LAST:, 1], ACT.Sqrt).then_inc(std_done, 1)

        def keep_x1T(k):
            act.wait_ge(tr_wr, k + 1)
            nc.scalar.copy(x1T[:, k, :], tr_ps[:, :]).then_inc(tr_rd, 1)

        def keep_router(g):
            act.wait_ge(lt_wr, g + 1)
            nc.scalar.copy(logitT, logit_ps[:, :]).then_inc(lt_kept, 1)

        def keep_logits(g):
            act.wait_ge(lg_wr, g + 1)
            nc.scalar.copy(logits[:, g * WAYS * ST:(g + 1) * WAYS * ST, :].rearrange("p (j t) e -> p t j e", t=ST),
                           rank_ps[:, :].rearrange("p (t j x) -> p t j x", t=ST, x=VW)[:, :, :, 0:EXP]).then_inc(lg_kept, 1)

        def gelus(at, width, bias, tiles=range(FC)):
            for f in tiles:
                act.wait_ge(h_wr, FC * at + f + 1)
                if f == 0 and at >= 2:
                    act.wait_ge(y_wr, at - 1)
                nc.scalar.activation(hidden[at % 2][:, f, 0:width], h_ps[:, f, 0:width], ACT.Gelu,
                                     bias=bias[:, f:f + 1]).then_inc(h_rd, 1)

        def keep_y(k):
            act.wait_ge(y_wr, place(k) + 1)
            nc.scalar.copy(y_fb[:, chunk_tiles(k), :], y_ps[:, :].rearrange("p (t e) -> p t e", t=ST)
                           ).then_inc(y_rd, 1)

        for g in range(GROUPS):
            k = g * WAYS
            for j in range(WAYS):
                keep_x1T(k + j)
                if g != 2:
                    gelus(min(g, 2), S, fb1, [j])
                if j == 1 and g > 0:
                    keep_logits(g - 1)
            keep_router(g)
            if g == 2:
                keep_y(0)
        keep_logits(GROUPS - 1)
        keep_y(1)
        for k in range(3, EARLY):
            gelus(k, S, fb1)
            keep_y(k - 1)
            if k == RANK_AT[0] // 4 + 1:
                act.wait_ge(zc_done, 1)
                nc.scalar.activation(cand[:, :, :], zc[:, :, :], ACT.Exp).then_inc(logit_e, 1)
                nc.scalar.activation(e2[:, :], e2[:, :], ACT.Exp).then_inc(logit_e, 1)
        keep_y(EARLY - 1)

        def keep_T(e):
            act.wait_ge(tr_wr, CHUNKS + e + 1)
            nc.scalar.copy(gatheredT[:, e * ET:(e + 1) * ET, :].rearrange("p t e -> p (t e)")[:, 0:CAP],
                           tr_b[e % 2][:, 0:CAP]).then_inc(tr_rd, 1)

        act.wait_ge(ld_exp, N_EXP)
        keep_T(0)
        for e in range(EXP):
            if e + 1 < EXP:
                keep_T(e + 1)
            gelus(EARLY + e, CAP, b1[:, e, :])

        def roots(n):
            first, end = NORMS[n]
            ts = slice(first * ST, end * ST)
            act.wait_ge(aggr2_done, end)
            nc.scalar.activation(std[:, ts], moments[:, ts, 1], ACT.Sqrt, bias=eps_col[:, 0:1]).then_inc(std2_done, 1)

        def normalise(n):
            act.wait_ge(shift2_done, n + 1)
            for k in range(*NORMS[n]):
                for tile in range(k * ST, k * ST + NORM_TILES):
                    last = nc.scalar.activation(result[:, tile, :], sums[:, tile, :], ACT.Identity,
                                                scale=rstd[:, tile:tile + 1], bias=shift2[:, tile:tile + 1])
                last.then_inc(out_ready, 1)

        gelus(place(EARLY), S, fb1)
        for k in range(EARLY + 1, CHUNKS):
            gelus(place(k), S, fb1)
            keep_y(k - 1)
        roots(0)
        normalise(0)
        keep_y(CHUNKS - 1)
        for n in range(1, len(NORMS)):
            roots(n)
            normalise(n)

    @block.vector
    def _(dve):
        done = [0]

        def step(ins):
            done[0] += 1
            ins.then_inc(v, 1)
            dve.wait_ge(v, done[0])

        def each(col, n=EXP):
            return col.unsqueeze(2).to_broadcast([P, TILES, n])

        def both(col):
            return col[:, :].unsqueeze(1).to_broadcast([P, 2, TILES])

        vec = nc.vector
        dve.sem_inc(x1_ready, NORMED)
        dve.wait_ge(std_done, 1)
        step(vec.reciprocal(rstd[:, LAST:], std[:, LAST:]))

        with dve.Fori(NORMED // 2, CHUNKS // 2) as i:
            for j in range(2):
                for t in range(ST):
                    tile = bass.ds((2 * i + j) * ST + t, 1)
                    row = z[:, tile, :].rearrange("p a e -> p (a e)")
                    last = vec.tensor_scalar(row, row, moments[:, tile, 0:1].rearrange("p a e -> p (a e)"), rstd[:, tile],
                                             ALU.subtract, ALU.mult)
                last.then_inc(x1_ready, 1)

        dve.wait_ge(ld_const, N_CONST)
        vec.tensor_copy(upto[:, :], upto_f[:, :])
        for c in (0, 1):
            step(vec.tensor_copy(learn[c][:, :, 0:2], token_f[:, :, :]))
        vec.memset(eps_col[:, :], EPS)
        vec.memset(zeros[:, :], 0.0)
        step(vec.memset(free[:, :], 1.0))

        dve.wait_ge(lg_kept, GROUPS)
        wide = order[:, :].unsqueeze(1).to_broadcast([P, TILES, EXP])
        step(vec.tensor_reduce(m1[:, :], logits[:, :, :], AX.X, ALU.max))
        step(vec.tensor_tensor(zc[:, :, :], logits[:, :, :], each(m1[:, :]), ALU.subtract))
        step(vec.tensor_scalar(zc[:, :, :], zc[:, :, :], -104.0, None, ALU.max))
        step(vec.scalar_tensor_tensor(cand[:, :, :], zc[:, :, :], 0.0, wide, ALU.is_equal, ALU.mult))
        step(vec.tensor_reduce(m1[:, :], cand[:, :, :], AX.X, ALU.max))
        step(vec.tensor_tensor(oh1[:, :, :], cand[:, :, :], each(m1[:, :]), ALU.is_equal))
        step(vec.scalar_tensor_tensor(slot_of[:, :, :], oh1[:, :, :], -1000.0, zc[:, :, :], ALU.mult, ALU.add))
        step(vec.tensor_reduce(e2[:, :], slot_of[:, :, :], AX.X, ALU.max))
        step(vec.tensor_tensor(cand[:, :, :], slot_of[:, :, :], each(e2[:, :]), ALU.is_equal))
        step(vec.tensor_tensor(cand[:, :, :], cand[:, :, :], wide, ALU.mult))
        step(vec.tensor_reduce(m1[:, :], cand[:, :, :], AX.X, ALU.max))
        step(vec.tensor_tensor(oh2[:, :, :], cand[:, :, :], each(m1[:, :]), ALU.is_equal))
        dve.sem_inc(zc_done, 1)

        for e in range(EXP):
            step(vec.tensor_tensor(elig[:, :], oh1[:, :, e], oh2[:, :, e], ALU.add))
            step(vec.tensor_tensor(elig[:, :], elig[:, :], free[:, :], ALU.mult))
            vec.tensor_copy(elig_b[:, :], elig[:, :])
            step(vec.tensor_tensor_scan(before[:, :], elig[:, :], zeros[:, :], 0.0, ALU.add, ALU.add))
            vec.tensor_tensor(before_b[:, :], before[:, :], elig[:, :], ALU.subtract).then_inc(elig_done, 1)
            if e == EXP - 5:
                dve.wait_ge(logit_e, 2)
                step(vec.tensor_reduce(sum8[:, :], cand[:, :, :], AX.X, ALU.add))
            elif e == EXP - 4:
                step(vec.reciprocal(score[:, 0, :], sum8[:, :]))
                step(vec.tensor_tensor(score[:, 1, :], score[:, 0, :], e2[:, :], ALU.mult))
            elif e == EXP - 3:
                step(vec.tensor_tensor(den[:, :], score[:, 0, :], score[:, 1, :], ALU.add))
                step(vec.tensor_scalar(den[:, :], den[:, :], 1e-9, None, ALU.max))
            elif e == EXP - 2:
                step(vec.reciprocal(den[:, :], den[:, :]))
            elif e == EXP - 1:
                step(vec.tensor_tensor(score[:, :, :], score[:, :, :], both(den), ALU.mult))
            dve.wait_ge(rank_wr, e + 1)
            step(vec.scalar_tensor_tensor(keep[:, :], rank_ps[:, 0:TILES], float(CAP), elig[:, :], ALU.is_le, ALU.mult))
            vec.scalar_tensor_tensor(slot_of[:, :, e], rank_ps[:, 0:TILES], float(e * ET * P), keep[:, :], ALU.add, ALU.mult)
            step(vec.tensor_tensor(elig[:, :], elig[:, :], keep[:, :], ALU.subtract))
            step(vec.tensor_tensor(free[:, :], free[:, :], elig[:, :], ALU.subtract))

        vec.tensor_scalar(over[:, :], free[:, :], -1.0, 1.0, ALU.mult, ALU.add)
        vec.tensor_tensor(score[:, :, :], score[:, :, :], both(free), ALU.mult)
        vec.tensor_tensor(zc[:, :, :], slot_of[:, :, :], oh1[:, :, :], ALU.mult)
        step(vec.tensor_tensor(oh2[:, :, :], slot_of[:, :, :], oh2[:, :, :], ALU.mult))
        vec.tensor_reduce(slot_c[:, 0, :], zc[:, :, :], AX.X, ALU.add)
        vec.tensor_reduce(slot_c[:, 1, :], oh2[:, :, :], AX.X, ALU.add)
        step(vec.tensor_copy(parts[:, :, :, 2], score[:, :, :]))
        step(vec.tensor_tensor(score[:, :, :], score[:, :, :], parts[:, :, :, 2], ALU.subtract))
        vec.tensor_scalar(taken[:, :, :], slot_c[:, :, :], 0.0, None, ALU.is_gt)
        step(vec.tensor_copy(parts[:, :, :, 3], score[:, :, :]))
        vec.tensor_tensor(score[:, :, :], score[:, :, :], parts[:, :, :, 3], ALU.subtract)
        step(vec.scalar_tensor_tensor(taken[:, :, :], taken[:, :, :], -NOWHERE - 1.0, slot_c[:, :, :], ALU.mult, ALU.add))
        vec.tensor_copy(parts[:, :, :, 4], score[:, :, :])
        step(vec.tensor_scalar(taken[:, :, :], taken[:, :, :], NOWHERE, None, ALU.add))
        step(vec.tensor_copy(slot_u[:, :, :], taken[:, :, :]))
        vec.tensor_scalar(lo_u[:, :, :], slot_u[:, :, :], P - 1, None, ALU.bitwise_and)
        step(vec.tensor_scalar(hi_u[:, :, :], slot_u[:, :, :], P.bit_length() - 1, None, ALU.logical_shift_right))
        vec.tensor_copy(lo_c[:, :, :], lo_u[:, :, :])
        step(vec.tensor_copy(hi_c[:, :, :], hi_u[:, :, :]))

        def add_fb(k):
            dve.wait_ge(fb_done, k + 1)
            for t in range(ST):
                tile = z[:, bass.ds(k * ST + t, 1), :].rearrange("p a e -> p (a e)")
                yt = y_fb[:, bass.ds(k * ST + t, 1), :].rearrange("p a e -> p (a e)")
                last = vec.scalar_tensor_tensor(tile, yt, over[:, bass.ds(k * ST + t, 1)], tile, ALU.mult, ALU.add)
            last.then_inc(sum_ready, 1)

        for n in range(NHOT):
            c, t0 = n // (NHOT // 2), n % (NHOT // 2) * ONE_HOT
            ts = slice(t0, t0 + ONE_HOT)
            if n >= 2:
                dve.wait_ge(hot_used, n - 1)
            lo = lo_c[:, c, ts].unsqueeze(2).to_broadcast([P, ONE_HOT, P])
            hot = one_hi[n % 2]
            hi = hi_c[:, c, ts].unsqueeze(2).to_broadcast([P, ONE_HOT, SLOT_TILES])
            vec.tensor_tensor(hot[:, :, :, 0], hi, slot_hi[:, :].unsqueeze(1).to_broadcast([P, ONE_HOT, SLOT_TILES]),
                              ALU.is_equal).then_inc(hi_done, 1)
            vec.tensor_tensor(one_lo[n % 2], lo, slot_lo[:, :].unsqueeze(1).to_broadcast([P, ONE_HOT, P]), ALU.is_equal)
            dve.wait_ge(hi_done, n + 1)
            vec.tensor_tensor(hot[:, :, :, 1:3], hot[:, :, :, 0:1].to_broadcast([P, ONE_HOT, SLOT_TILES, 2]),
                              learn[c][:, ts, 0:2].unsqueeze(2).to_broadcast([P, ONE_HOT, SLOT_TILES, 2]),
                              ALU.mult).then_inc(hot_done, 1)
        dve.wait_ge(hot_used, NHOT)
        step(vec.tensor_copy(found[:, :, :], hot_ps.rearrange("p (t v) -> p t v", v=NV)))
        step(vec.scalar_tensor_tensor(dest[:, :], found[:, :, 1], float(P), found[:, :, 2], ALU.mult, ALU.add))
        vec.tensor_copy(from_row[:, :], dest[:, :])
        step(vec.tensor_tensor(tmp_s[:, :], found[:, :, 0], spare[:, :], ALU.mult))
        step(vec.tensor_tensor(tmp_s[:, :], spare[:, :], tmp_s[:, :], ALU.subtract))
        step(vec.tensor_tensor(tmp_s[:, :], tmp_s[:, :], dest[:, :], ALU.add))
        step(vec.tensor_copy(to_row[:, :], tmp_s[:, :]))
        step(vec.tensor_tensor(slot_w[:, :], found[:, :, 4], found[:, :, 5], ALU.add))
        vec.tensor_tensor(slot_w[:, :], slot_w[:, :], found[:, :, 3], ALU.add).then_inc(rows_done, 1)
        dve.wait_ge(x1_out, 16 * CHUNKS)
        with dve.Fori(0, EARLY // 2) as i:
            for j in range(2):
                add_fb(2 * i + j)

        dve.wait_ge(rows_done, 1)
        dve.wait_ge(ld_exp, N_EXP)
        for e in range(EXP):
            dve.wait_ge(y_wr, EARLY + e + 1)
            y = y_e[e % 2][:, :].rearrange("p (t e) -> p t e", e=E)
            vec.tensor_tensor(gathered[:, e * ET:e * ET + FULL, :], y[:, 0:FULL, :],
                              b2[:, e:e + 1, :].to_broadcast([P, FULL, E]), ALU.add)
            n = ET_ROWS[-1]
            step(vec.tensor_tensor(gathered[0:n, e * ET + FULL, :], y[0:n, FULL, :], b2[0:n, e, :], ALU.add))
            for t in range(ET):
                n = ET_ROWS[t]
                s = e * ET + t
                last = vec.tensor_scalar(gathered[0:n, s, :], gathered[0:n, s, :], slot_w[0:n, s:s + 1], None, ALU.mult)
            last.then_inc(weighed, 1)

        def add_late(k):
            dve.wait_ge(fb_done, k + 1)
            for tile in range(k * ST, (k + 1) * ST):
                last = vec.scalar_tensor_tensor(sums[:, tile, :], y_fb[:, tile, :], over[:, tile:tile + 1], sums[:, tile, :],
                                                ALU.mult, ALU.add)
            step(last)

        def aggregate(k):
            dve.wait_ge(stats2_done, k + 1)
            for t in range(k * ST, (k + 1) * ST):
                last = vec.bn_aggr(moments[:, t, :], stats2[:, t, :])
            last.then_inc(aggr2_done, 1)

        def scale_and_shift(n):
            ts = slice(NORMS[n][0] * ST, NORMS[n][1] * ST)
            dve.wait_ge(std2_done, n + 1)
            step(vec.reciprocal(rstd[:, ts], std[:, ts]))
            vec.scalar_tensor_tensor(shift2[:, ts], moments[:, ts, 0], -1.0, rstd[:, ts], ALU.mult, ALU.mult
                                     ).then_inc(shift2_done, 1)

        for n, (first, end) in enumerate(NORMS):
            for k in range(first, end):
                dve.wait_ge(sum_load[k], 16)
                if k >= EARLY:
                    add_late(k)
                for t in range(k * ST, (k + 1) * ST):
                    last = vec.bn_stats(stats2[:, t, :], sums[:, t, :])
                last.then_inc(stats2_done, 1)
                if k > first:
                    aggregate(k - 1)
                if k in SCALE_AT:
                    scale_and_shift(SCALE_AT[k])
            aggregate(end - 1)
        scale_and_shift(len(NORMS) - 1)


def program(nc, x, w_qkv, w_out, w, out):
    with (nc.sbuf_tensor("z", [P, TILES, E], F32) as z, nc.sbuf_tensor("moments", [P, TILES, 2], F32) as moments,
          nc.sbuf_tensor("std", [P, TILES], F32) as std, nc.sbuf_tensor("rstd", [P, TILES], F32) as rstd,
          nc.sbuf_tensor("ident", [P, P], F32) as ident,
          nc.sbuf_tensor("w_r", [P, VW], F32) as w_r,
          nc.sbuf_tensor("fw1_sb", [P, FF], F32) as fw1, nc.sbuf_tensor("fb1_sb", [P, FC], F32) as fb1):
        with ExitStack() as ctx:
            block = ctx.enter_context(nc.Block())
            nc.disable_value_cache = True
            attention(nc, ctx, block, x, w_qkv, w_out, ident, w["ident"], z, moments, std, rstd, w_r,
                      ((w_r[:, 0:EXP], w["Wr"]), (fw1[:, :], w["fw1"]), (fb1[:, :], w["fb1"])))
            nc.disable_value_cache = False
        with ExitStack() as ctx:
            block = ctx.enter_context(nc.Block())
            feed_forward(nc, ctx, block, w, ident, z, moments, std, rstd, w_r, fw1, fb1, out)


_INPUTS = ["L0_attn_x", "L0_attn_w_qkv", "L0_attn_w_out", "L0_ffn_Wr", "L0_ffn_W1", "L0_ffn_W2", "L0_ffn_fw1",
           "L0_ffn_fw2", "L0_ffn_fb2"]


def kernel(**inputs):
    import numpy as np
    import concourse.bacc as bacc
    from concourse.bass_utils import run_bass_kernel_spmd

    arrays = {name: np.ascontiguousarray(inputs[name]) for name in _INPUTS}
    arrays["fb1"] = np.ascontiguousarray(np.asarray(inputs["L0_ffn_fb1"]).reshape(FC, P).T)
    arrays["b1"] = np.ascontiguousarray(np.asarray(inputs["L0_ffn_b1"]).reshape(EXP, FC, P).transpose(2, 0, 1))
    arrays["b2"] = np.ascontiguousarray(inputs["L0_ffn_b2"])
    w_qkv = np.asarray(inputs["L0_attn_w_qkv"]).reshape(E, 3, H, D)
    arrays["L0_attn_w_qkv"] = np.concatenate([w_qkv[:, 0:2].swapaxes(2, 3).reshape(E, 2 * E),
                                              w_qkv[:, 2].reshape(E, E)], axis=1)
    arrays["ident"] = np.eye(P, dtype=np.float32)
    arrays["upto"] = np.triu(np.ones((P, P), np.float32))
    arrays["order"] = np.tile(np.arange(EXP, 0, -1, dtype=np.float32), (P, 1))
    arrays["slot_lo"] = np.tile(np.arange(P, dtype=np.float32), (P, 1))
    arrays["slot_hi"] = np.tile(np.arange(SLOT_TILES, dtype=np.float32), (P, 1))
    no = np.zeros((P, TILES, 2), np.float32)
    no[:, :, 0] = np.arange(TILES)
    no[:, :, 1] = np.arange(P)[:, None]
    arrays["token_no"] = no
    own = np.arange(SLOT_TILES)[None, :] % ET * P + np.arange(P)[:, None]
    arrays["spare"] = (TOK + own).astype(np.float32)

    nc = bacc.Bacc("TRN2", target_bir_lowering=False, num_devices=1)
    aps = {name: nc.dram_tensor("in_" + name, a.shape, mybir.dt.from_np(a.dtype), kind="ExternalInput").ap()
           for name, a in arrays.items()}
    out = nc.dram_tensor("out_0", (BATCH, S, E), F32, kind="ExternalOutput").ap()
    w = {name.replace("L0_ffn_", ""): ap for name, ap in aps.items()}
    program(nc, aps["L0_attn_x"], aps["L0_attn_w_qkv"], aps["L0_attn_w_out"], w, out)
    r = run_bass_kernel_spmd(nc, [{"in_" + name: a for name, a in arrays.items()}], core_ids=[0])
    return r.results[0]["out_0"]
```
